# Optimizing a Trainium2 kernel written in Bass

```python
import numpy as np
import jax
import jax.numpy as jnp

def _softmax(x, axis=-1):
    return jax.nn.softmax(x, axis=axis)

def _gelu(x):
    return jax.nn.gelu(x, approximate=True)

def _silu(x):
    return jax.nn.silu(x)

def _sigmoid(x):
    return jax.nn.sigmoid(x)

def _layernorm(x, axis=-1, eps=1e-05):
    m = jnp.mean(x, axis=axis, keepdims=True)
    v = jnp.var(x, axis=axis, keepdims=True)
    return (x - m) / jnp.sqrt(v + eps)

def _scatter_add(tgt, idx, src, axis=0):
    return tgt.at[idx].add(src)

def _segment_sum(src, seg, n):
    return jax.ops.segment_sum(src, seg, n)
kernel_name = 'mk_gnn_ffn_d1_gnn_r32_d8bacd'

def setup_inputs(seed: int=0):
    np.random.seed(seed)
    _w = jnp.asarray

    def _rec_inputs():
        import jax
        import jax.numpy as jnp
        _gk = jax.random.key(seed)
        x = -0.0005963 + 1.001 * jax.random.normal(jax.random.fold_in(_gk, 1), (96, 1024), jnp.float32)
        _s = jax.random.randint(jax.random.fold_in(_gk, 2), (1536,), 0, 96, jnp.int32)
        _d = jax.random.randint(jax.random.fold_in(_gk, 3), (1536,), 0, 96, jnp.int32)
        _loop = jnp.arange(96, dtype=jnp.int32)
        src = jnp.concatenate([_s, _d, _loop])
        dst = jnp.concatenate([_d, _s, _loop])
        _o = jnp.argsort(dst, stable=True)
        src = src[_o]
        dst = dst[_o]
        edge_type_5 = jax.random.randint(jax.random.fold_in(_gk, 12), (3168,), 0, 5, jnp.int32)
        return (x, src, dst, edge_type_5)
    x, src, dst, edge_type_5 = _rec_inputs()

    def _L0_gnn_setup():
        import jax, jax.numpy as jnp
        import numpy as np
        N = 96
        E = 3072
        IN_F = 1024
        OUT_F = 1024
        H = 16
        D = OUT_F // H
        NUM_ETYPES = 4

        def _build_mask(edge_index, edge_type, edge_type_weights, dtype):
            src, dst = (edge_index[0], edge_index[1])
            w = jax.nn.softplus(edge_type_weights)
            mask = jnp.full((N, N), -jnp.inf, dtype=dtype)
            mask = mask.at[src, dst].set(w[edge_type - 1])
            diag = jnp.diagonal(mask)
            idx = jnp.arange(N)
            mask = mask.at[idx, idx].set(jnp.where(jnp.isneginf(diag), w[3], diag))
            return mask
        key = jax.random.key(seed)
        ks = jax.random.split(key, 20)
        p = lambda k, shape: jax.random.normal(k, shape, dtype=jnp.float32) * 0.02
        return {'x': jax.random.normal(ks[0], (N, IN_F), dtype=jnp.float32), 'edge_index': jax.random.randint(ks[1], (2, E), 0, N), 'edge_type': jax.random.randint(ks[2], (E,), 1, NUM_ETYPES + 1), 'edge_type_weights': jnp.ones((NUM_ETYPES,), jnp.float32) + 0.1 * jax.random.normal(ks[3], (NUM_ETYPES,), dtype=jnp.float32), 'wq': p(ks[4], (OUT_F, IN_F)), 'bq': p(ks[5], (OUT_F,)), 'wk': p(ks[6], (OUT_F, IN_F)), 'bk': p(ks[7], (OUT_F,)), 'wv': p(ks[8], (OUT_F, IN_F)), 'bv': p(ks[9], (OUT_F,)), 'wiq': p(ks[10], (OUT_F, OUT_F)), 'biq': p(ks[11], (OUT_F,)), 'wik': p(ks[12], (OUT_F, OUT_F)), 'bik': p(ks[13], (OUT_F,)), 'wiv': p(ks[14], (OUT_F, OUT_F)), 'biv': p(ks[15], (OUT_F,)), 'wo': p(ks[16], (OUT_F, OUT_F)), 'bo': p(ks[17], (OUT_F,))}
    _L0_gnn_all = _L0_gnn_setup()
    _L0_gnn_in = {k: v for k, v in _L0_gnn_all.items() if k in ('edge_type_weights', 'wq', 'bq', 'wk', 'bk', 'wv', 'bv', 'wiq', 'biq', 'wik', 'bik', 'wiv', 'biv', 'wo', 'bo')}
    del _L0_gnn_all

    def _L0_ffn_setup():
        import jax, jax.numpy as jnp
        import numpy as np
        D_MODEL = 1024
        NUM_EXPERTS = 8
        TOP_K = 2
        key = jax.random.key(seed)
        k_x, k_g, k_w1, k_w2 = jax.random.split(key, 4)
        B, S, D, E = (4, 64, D_MODEL, NUM_EXPERTS)
        s_in = 1.0 / np.sqrt(D)
        s_hid = 1.0 / np.sqrt(4 * D)
        return {'x': jax.random.normal(k_x, (B, S, D), dtype=jnp.float32), 'gate_w': jax.random.uniform(k_g, (E, D), jnp.float32, -s_in, s_in), 'w1': jax.random.uniform(k_w1, (E, 4 * D, D), jnp.float32, -s_in, s_in), 'w2': jax.random.uniform(k_w2, (E, D, 4 * D), jnp.float32, -s_hid, s_hid)}
    _L0_ffn_all = _L0_ffn_setup()
    _L0_ffn_in = {k: v for k, v in _L0_ffn_all.items() if k in ('gate_w', 'w1', 'w2')}
    del _L0_ffn_all
    return {'x': x, 'src': src, 'dst': dst, 'edge_type_5': edge_type_5, 'L0_gnn_edge_type_weights': _L0_gnn_in['edge_type_weights'], 'L0_gnn_wq': _L0_gnn_in['wq'], 'L0_gnn_bq': _L0_gnn_in['bq'], 'L0_gnn_wk': _L0_gnn_in['wk'], 'L0_gnn_bk': _L0_gnn_in['bk'], 'L0_gnn_wv': _L0_gnn_in['wv'], 'L0_gnn_bv': _L0_gnn_in['bv'], 'L0_gnn_wiq': _L0_gnn_in['wiq'], 'L0_gnn_biq': _L0_gnn_in['biq'], 'L0_gnn_wik': _L0_gnn_in['wik'], 'L0_gnn_bik': _L0_gnn_in['bik'], 'L0_gnn_wiv': _L0_gnn_in['wiv'], 'L0_gnn_biv': _L0_gnn_in['biv'], 'L0_gnn_wo': _L0_gnn_in['wo'], 'L0_gnn_bo': _L0_gnn_in['bo'], 'L0_ffn_gate_w': _L0_ffn_in['gate_w'], 'L0_ffn_w1': _L0_ffn_in['w1'], 'L0_ffn_w2': _L0_ffn_in['w2']}

def reference(x, src, dst, edge_type_5, L0_gnn_edge_type_weights, L0_gnn_wq, L0_gnn_bq, L0_gnn_wk, L0_gnn_bk, L0_gnn_wv, L0_gnn_bv, L0_gnn_wiq, L0_gnn_biq, L0_gnn_wik, L0_gnn_bik, L0_gnn_wiv, L0_gnn_biv, L0_gnn_wo, L0_gnn_bo, L0_ffn_gate_w, L0_ffn_w1, L0_ffn_w2):
    import jax
    import jax.numpy as jnp

    def _L0_gnn_ref(x, edge_index, edge_type, edge_type_weights, wq, bq, wk, bk, wv, bv, wiq, biq, wik, bik, wiv, biv, wo, bo):
        import jax, jax.numpy as jnp
        import numpy as np
        N = 96
        E = 3072
        IN_F = 1024
        OUT_F = 1024
        H = 16
        D = OUT_F // H
        NUM_ETYPES = 4

        def _build_mask(edge_index, edge_type, edge_type_weights, dtype):
            src, dst = (edge_index[0], edge_index[1])
            w = jax.nn.softplus(edge_type_weights)
            mask = jnp.full((N, N), -jnp.inf, dtype=dtype)
            mask = mask.at[src, dst].set(w[edge_type - 1])
            diag = jnp.diagonal(mask)
            idx = jnp.arange(N)
            mask = mask.at[idx, idx].set(jnp.where(jnp.isneginf(diag), w[3], diag))
            return mask
        q = x @ wq.T + bq
        k = x @ wk.T + bk
        v = x @ wv.T + bv
        q2 = (q @ wiq.T + biq).reshape(N, H, D).transpose(1, 0, 2)
        k2 = (k @ wik.T + bik).reshape(N, H, D).transpose(1, 0, 2)
        v2 = (v @ wiv.T + biv).reshape(N, H, D).transpose(1, 0, 2)
        mask = _build_mask(edge_index, edge_type, edge_type_weights, x.dtype)
        scale = 1.0 / np.sqrt(D).astype(np.float32)
        scores = jnp.einsum('hnd,hmd->hnm', q2, k2) * scale + mask[None]
        attn = jax.nn.softmax(scores, axis=-1)
        out = jnp.einsum('hnm,hmd->hnd', attn, v2)
        out = out.transpose(1, 0, 2).reshape(N, OUT_F)
        return out @ wo.T + bo

    def _L0_ffn_ref(x, gate_w, w1, w2):
        import jax, jax.numpy as jnp
        import numpy as np
        D_MODEL = 1024
        NUM_EXPERTS = 8
        TOP_K = 2
        gate_logits = jnp.einsum('bsd,ed->bse', x, gate_w)
        top_v, top_i = jax.lax.top_k(gate_logits, TOP_K)
        gates = jax.nn.softmax(top_v, axis=-1)
        combine = jnp.sum(jax.nn.one_hot(top_i, NUM_EXPERTS, dtype=x.dtype) * gates[..., None], axis=-2)
        out = jnp.zeros_like(x)
        for e in range(NUM_EXPERTS):
            h = jax.nn.relu(jnp.einsum('bsd,fd->bsf', x, w1[e]))
            y = jnp.einsum('bsf,df->bsd', h, w2[e])
            out = out + combine[..., e, None] * y
        return out
    edge_index = jnp.stack([src, dst])
    x = x + _L0_gnn_ref(_layernorm(x, axis=-1), edge_index, edge_type_5, L0_gnn_edge_type_weights, L0_gnn_wq, L0_gnn_bq, L0_gnn_wk, L0_gnn_bk, L0_gnn_wv, L0_gnn_bv, L0_gnn_wiq, L0_gnn_biq, L0_gnn_wik, L0_gnn_bik, L0_gnn_wiv, L0_gnn_biv, L0_gnn_wo, L0_gnn_bo)
    x = x + _L0_ffn_ref(_layernorm(x, axis=-1)[None], L0_ffn_gate_w, L0_ffn_w1, L0_ffn_w2)[0]
    return x

_drawn_inputs = setup_inputs


def setup_inputs(seed=0):
    import zlib

    import numpy as np

    out = dict(_drawn_inputs(seed))
    spreads = {}
    factors = {'L0_gnn_edge_type_weights': 8.0,
     'L0_gnn_wq': 2.793,
     'L0_gnn_bq': 8.0,
     'L0_gnn_wk': 6.703,
     'L0_gnn_bk': 64.0,
     'L0_gnn_bv': 3.242,
     'L0_gnn_wiq': 2.795,
     'L0_gnn_biq': 8.0,
     'L0_gnn_wik': 3.181,
     'L0_gnn_bik': 64.0,
     'L0_gnn_biv': 2.723}
    for name, (base, spread) in spreads.items():
        noise = np.random.default_rng([zlib.crc32(name.encode()), seed]).standard_normal(out[name].shape)
        drawn = base * np.exp(spread * noise) if base else spread * noise
        out[name] = jnp.asarray(drawn.astype(out[name].dtype))
    for name, factor in factors.items():
        out[name] = (out[name] * factor).astype(out[name].dtype)
    return out
```

```python
from contextlib import ExitStack

import numpy as np

import concourse.bass as bass
from concourse import mybir

F32 = mybir.dt.float32
F16 = mybir.dt.float16
I32 = mybir.dt.int32
ALU = mybir.AluOpType
ACT = mybir.ActivationFunctionType
AX = mybir.AxisListType

P = 128
N = 96
D = 1024
KT = D // P
HEADS = 16
HD = D // HEADS
E = 8
F = 4 * D
EDGES = 3168
EC = EDGES // N
EG = 5
NG = -(-EC // EG)
HALF = 512
SLOTS = 32
OVER = (2 * N) // (SLOTS + 1)
JOBS = E + OVER + 1
UNITS = 2
UF = F // UNITS
CT = UF // P // 4
CHUNK = 4096
W1C = KT * UF // CHUNK
W2C = (UF // P) * D // CHUNK
RING = 8
EXTRA = 2
GSLOTS = RING + EXTRA
PER_JOB = UNITS * (W1C + W2C)
EPS = 1e-5
FAR = -1e30
SCALE = 1.0 / 8.0
SHIFT = 8
assert EC * N == EDGES and W1C + W2C == RING and HD * HEADS == D and SCALE * SCALE * HD == 1.0
assert UF == 4 * HALF and CT * 4 * P == UF and JOBS * SLOTS <= HALF

Q, K, Q2, V, K2, V2, O = range(7)
NGC = 14


def gslot(g):
    return (g + GSLOTS - 4) % GSLOTS


def gnn_moe_kernel(nc, x_d, rows_d, cols_d, etw_d, gnn_w_d, colb_d, biv_d, bo_d, gate_d, w1_d, w2_d, out_d):
    with ExitStack() as ctx:
        def sb(name, shape, dt=F32):
            return ctx.enter_context(nc.sbuf_tensor(name, shape, dt))

        def sem(name):
            return ctx.enter_context(nc.semaphore(name))

        ring = sb("ring", [P, GSLOTS * CHUNK])

        def slot(s, n=1):
            return ring[:, s * CHUNK:(s + n) * CHUNK]

        rows_i = slot(3)[0:2, 0:EDGES].bitcast(I32)
        early = slot(4, 2).bitcast(F16)
        rows16 = early[0:2, 0:EDGES]
        same = early[0:N, EDGES:2 * EDGES].rearrange("p (t j) -> p t j", j=N)
        src1h = early[0:N, 2 * EDGES:3 * EDGES].rearrange("p (t j) -> p t j", j=N)
        dst1h = early[0:N, 3 * EDGES:4 * EDGES].rearrange("p (t j) -> p t j", j=N)
        late = slot(RING, EXTRA)
        o0 = KT * JOBS * SLOTS
        o1 = o0 + JOBS * N
        o2 = o1 + JOBS * P
        o3 = o2 + JOBS * SLOTS
        o4 = o3 + KT * SLOTS
        xg_all = late[:, 0:o0].rearrange("p (k j s) -> p k j s", k=KT, s=SLOTS)
        sc_all = late[:, o0:o1].rearrange("p (j n) -> p j n", n=N)
        selg = late[0:N, o1:o2].rearrange("p (j c s) -> p j c s", j=JOBS, s=SLOTS)
        sel = late[0:N, o2:o3].rearrange("p (j s) -> p j s", s=SLOTS)
        xg = late[:, o3:o4].rearrange("p (k s) -> p k s", s=SLOTS)
        sc = late[:, o4:o4 + N]
        assert o4 + N <= EXTRA * CHUNK

        x = sb("x", [N, D])
        xn = sb("xn", [N, D])
        x2 = sb("x2", [N, D])
        xT = sb("xT", [P, KT, N])
        qvT = sb("qvT", [P, KT, N])
        koT = sb("koT", [P, KT, N])
        qk2T = sb("qk2T", [P, 2 * KT * N])
        q2Tv = qk2T[:, 0:KT * N].rearrange("p (k n) -> p k n", n=N)
        k2Tv = qk2T[:, KT * N:].rearrange("p (k n) -> p k n", n=N)
        v2 = qk2T[0:N, 0:D]
        attn = sb("attn", [P, HEADS * N])
        attnT = sb("attnT", [P, HEADS * N])
        attnv = attn[0:N, :].rearrange("p (h m) -> p h m", m=N)
        attnTv = attnT[0:N, :].rearrange("p (h m) -> p h m", m=N)
        h_s = qvT[:, :, :].rearrange("p k n -> p (k n)")[:, 0:HALF]
        h_T = koT[:, :, :].rearrange("p k n -> p (k n)")[:, 0:HALF]
        y_s = attn[:, 0:D]
        out_s = attnT[0:N, 0:D]

        ident = sb("ident", [P, P])
        upper = sb("upper", [N, N])
        ones = sb("ones", [N, N])
        tri16 = sb("tri16", [N, N], F16)
        iota_i = sb("iota_i", [N, N], I32)
        iota_f = sb("iota_f", [N, N])
        iota16 = sb("iota16", [N, N], F16)
        code_i = sb("code_i", [N, EC], I32)
        pair16 = sb("pair16", [2, N], F16)
        cols_i = sb("cols_i", [N, 3, EC], I32)
        cols = sb("cols", [N, 3, EC])
        cols16 = sb("cols16", [N, 3, EC], F16)
        ec = sb("ec", [N, 6, EC])
        kv16 = sb("kv16", [N, EC], F16)
        merged, mtmp = attnT[0:N, 0:N], attnT[0:N, N:2 * N]
        mcode_i = attnT[0:N, 2 * N:3 * N].bitcast(I32)
        mask = sb("mask", [N, N])
        etw = sb("etw", [N, 4])
        sp = sb("sp", [N, 4, 4])
        colb = sb("colb", [P, 5, KT])
        gate_w = sb("gate_w", [P, KT, E])
        stat = sb("stat", [N, 2, 6])
        mv = sb("mv", [N, 2])
        std = sb("std", [N, 1])
        rstd = sb("rstd", [N, 1])
        smx = sb("smx", [N, 4, 4])
        ssum = sb("ssum", [N, 4, 4])
        rt = sb("rt", [N, 16, E])
        r1 = sb("r1", [N, 16])
        ov = sb("ov", [N, 4, OVER, E])
        kk = sb("kk", [N, OVER, E])
        jp = sb("jp", [N, JOBS])
        jg = sb("jg", [N, JOBS])
        ot = sb("ot", [N, 3, OVER])
        table = sb("table", [1, 1 + OVER], I32)

        bank = [ctx.enter_context(nc.psum_tensor(f"bank{b}", [P, HALF], F32)) for b in range(8)]
        ps_h, ps_t, ps_y, ps_o = bank[0], bank[1], bank[2:4], bank[4:6]

        def quarter(b, rows=P, n=4):
            return b[0:rows, :].rearrange("p (q c) -> p q c", c=P)[:, 0:n, 0:N]

        def edge_bank(b, t):
            return b[0:N, 0:t * N].rearrange("p (t j) -> p t j", j=N)

        def gather_bank(k):
            return bank[(0, 1, 6, 7)[k % 4]][:, 0:JOBS * SLOTS].rearrange("p (j s) -> p j s", s=SLOTS)

        x_in, rows_in, cols_in, etw_in, colb_in, gate_in, biv_in, bo_in = (
            sem(s) for s in ("x_in", "rows_in", "cols_in", "etw_in", "colb_in", "gate_in", "biv_in", "bo_in"))
        gnn_in = [sem(f"gnn_in{g}") for g in range(NGC)]
        ring_in = [sem(f"ring_in{s}") for s in range(RING)]
        gnn_used = sem("gnn_used")
        chunk_used = sem("chunk_used")
        const_ready = sem("const_ready")
        pool_step = sem("pool_step")
        dve_step = sem("dve_step")
        act_step = sem("act_step")
        rows_read = sem("rows_read")
        var_ready, std_ready = sem("var_ready"), sem("std_ready")
        xn_ready, xT_done, xT_ready = sem("xn_ready"), sem("xT_done"), sem("xT_ready")
        rows_ready = sem("rows_ready")
        cell_done, same_done = sem("cell_done"), sem("same_done")
        onehot_ready, kv_ready, code_ready = sem("onehot_ready"), sem("kv_ready"), sem("code_ready")
        map_done, map_read = sem("map_done"), sem("map_read")
        etw_exp, etw_ln = sem("etw_exp"), sem("etw_ln")
        etw_abs = sem("etw_abs")
        proj_read = sem("proj_read")
        score_done, score_sub, score_exp = sem("score_done"), sem("score_sub"), sem("score_exp")
        probs_ready, probsT_done, probsT_ready = sem("probs_ready"), sem("probsT_done"), sem("probsT_ready")
        v2_done, v2_ready = sem("v2_done"), sem("v2_ready")
        pv_done, oT_ready = sem("pv_done"), sem("oT_ready")
        o_done, x2_ready = sem("o_done"), sem("x2_ready")
        x3_ready, x3T_done, x3T_ready = sem("x3_ready"), sem("x3T_done"), sem("x3T_ready")
        logit_done, gap_ready, gap_exp = sem("logit_done"), sem("gap_ready"), sem("gap_exp")
        chosen_ready, rank_done = sem("chosen_ready"), sem("rank_done")
        sel_ready, gather_done, gather_read = sem("sel_ready"), sem("gather_done"), sem("gather_read")
        selg_ready, sct_done, sct_read = sem("selg_ready"), sem("sct_done"), sem("sct_read")
        table_ready = sem("table_ready")
        xg_ready, sc_ready = sem("xg_ready"), sem("sc_ready")
        h_ready, hT_done, hT_ready = sem("h_ready"), sem("hT_done"), sem("hT_ready")
        y_ready, scat_done = sem("y_ready"), sem("scat_done")
        out_ready, stored = sem("out_ready"), sem("stored")

        block = ctx.enter_context(nc.Block())

        @block.sync
        def _(sp_):
            sp_.dma_start(x[:, :], x_d).then_inc(x_in, 16)
            for g in range(NGC):
                if gslot(g) == 3:
                    sp_.wait_ge(rows_read, 1)
                if gslot(g) == 4:
                    sp_.wait_ge(map_done, NG)
                if g >= GSLOTS:
                    sp_.wait_ge(gnn_used, g - GSLOTS + 1)
                sp_.dma_start(slot(gslot(g)), gnn_w_d[g]).then_inc(gnn_in[g], 16)

            def expert_chunk(expert, c):
                u, r = c // RING, c % RING
                src = w1_d[expert, u, r] if r < W1C else w2_d[expert, u, r - W1C]
                sp_.dma_start(slot(r), src).then_inc(ring_in[r], 16)

            for c in range(PER_JOB):
                if c < RING:
                    sp_.wait_ge(gnn_used, c + 5)
                else:
                    sp_.wait_ge(chunk_used, c - RING + 1)
                expert_chunk(0, c)
            with sp_.Fori(1, E) as e:
                for c in range(PER_JOB):
                    sp_.wait_ge(chunk_used, e * PER_JOB + (c - RING + 1))
                    expert_chunk(e, c)
            sp_.wait_ge(table_ready, 1)
            jobs = sp_.value_load(table[0:1, 0:1], min_val=E, max_val=E + OVER)
            with sp_.If(jobs > E):
                with sp_.Fori(E, jobs) as job:
                    e = sp_.value_load(table[0:1, bass.ds(job - (E - 1), 1)], min_val=0, max_val=E - 1)
                    for c in range(PER_JOB):
                        sp_.wait_ge(chunk_used, job * PER_JOB + (c - RING + 1))
                        expert_chunk(e, c)
            sp_.wait_ge(out_ready, 2)
            sp_.dma_start(out_d, out_s).then_inc(stored, 16)
            sp_.wait_ge(stored, 16)

        @block.gpsimd
        def _(pool):
            pool.dma_start(cols_i[:, :, :], cols_d).then_inc(cols_in, 16)
            pool.memset(ones[:, :], 1.0).then_inc(pool_step, 1)
            pool.memset(ident[:, :], 1.0).then_inc(pool_step, 1)
            pool.memset(pair16[:, :], 1.0).then_inc(pool_step, 1)
            pool.iota(iota_i[:, :], [[1, N]], base=0, channel_multiplier=0).then_inc(pool_step, 1)
            pool.iota(code_i[:, :], [[SHIFT, EC]], base=0, channel_multiplier=0).then_inc(pool_step, 1)
            pool.wait_ge(pool_step, 5)
            pool.affine_select(out=ident[:, :], in_=ident[:, :], compare_op=ALU.is_equal, fill=0.0, base=0,
                               pattern=[[1, P]], channel_multiplier=-1).then_inc(const_ready, 1)
            pool.affine_select(out=upper[:, :], in_=ones[:, :], compare_op=ALU.is_gt, fill=0.0, base=0,
                               pattern=[[1, N]], channel_multiplier=-1).then_inc(const_ready, 1)
            pool.memset(pair16[0:1, :], float(N)).then_inc(const_ready, 1)
            pool.tensor_copy(iota_f[:, :], iota_i[:, :]).then_inc(const_ready, 1)
            pool.tensor_copy(iota16[:, :], iota_i[:, :]).then_inc(const_ready, 1)
            pool.wait_ge(const_ready, 5)
            pool.tensor_copy(tri16[:, :], upper[:, :]).then_inc(const_ready, 1)
            pool.wait_ge(onehot_ready, 2)
            pool.wait_ge(kv_ready, 1)
            pool.tensor_tensor(dst1h, dst1h, kv16[:, :, None].to_broadcast([N, EC, N]),
                               ALU.mult).then_inc(code_ready, 1)

        @block.scalar
        def _(act):
            act.dma_start(rows_i, rows_d).then_inc(rows_in, 16)
            act.dma_start(etw[:, :], etw_d.to_broadcast([N, 4])).then_inc(etw_in, 16)
            act.dma_start(colb[:, :, :], colb_d).then_inc(colb_in, 16)
            act.dma_start(gate_w[:, :, :], gate_d).then_inc(gate_in, 16)
            act.dma_start(x2[:, :], bo_d.to_broadcast([N, D])).then_inc(bo_in, 16)
            def root(n):
                act.wait_ge(var_ready, n)
                nc.scalar.activation(std[:, :], mv[:, 1:2], ACT.Sqrt, bias=EPS).then_inc(std_ready, 1)

            root(1)
            for b in range(2):
                act.wait_ge(xT_done, b + 1)
                nc.scalar.copy(xT[:, 4 * b:4 * b + 4, :], quarter(bank[b])).then_inc(xT_ready, 1)
            act.wait_ge(etw_abs, 1)
            nc.scalar.activation(sp[:, 1, :], sp[:, 0, :], ACT.Exp).then_inc(etw_exp, 1)
            act.wait_ge(etw_exp, 1)
            nc.scalar.activation(sp[:, 2, :], sp[:, 1, :], ACT.Ln, bias=1.0).then_inc(etw_ln, 1)
            act.wait_ge(colb_in, 16)
            banks = {Q: (2, 3), K: (4, 5), Q2: (6, 7), V: (2, 3), K2: (4, 5)}
            outs = {Q: qvT, K: koT, Q2: q2Tv, V: qvT, K2: k2Tv}
            for m in (Q, K, Q2, V, K2):
                for h in range(2):
                    act.wait_ge(gnn_used, 2 * m + h + 1)
                    for t in range(4):
                        last = nc.scalar.activation(outs[m][:, 4 * h + t, :], bank[banks[m][h]][:, P * t:P * t + N],
                                                    ACT.Identity, bias=colb[:, m, 4 * h + t:4 * h + t + 1])
                    last.then_inc(proj_read, 1)
            act.wait_ge(score_done, 4)
            act.dma_start(v2, biv_d.to_broadcast([N, D])).then_inc(biv_in, 16)
            for b in range(4):
                act.wait_ge(score_sub, b + 1)
                s = attnv[:, 4 * b:4 * b + 4, :]
                nc.scalar.activation(s, s, ACT.Exp).then_inc(score_exp, 1)
            for b in range(4):
                act.wait_ge(probsT_done, b + 1)
                nc.scalar.copy(attnTv[:, 4 * b:4 * b + 4, :], quarter(bank[(0, 1, 6, 7)[b]], N)).then_inc(probsT_ready, 1)
            for b in range(2):
                act.wait_ge(pv_done, b + 1)
                nc.scalar.copy(koT[:, 4 * b:4 * b + 4, :], quarter(bank[4 + b])).then_inc(oT_ready, 1)
            root(2)
            act.wait_ge(x3T_done, 1)
            nc.scalar.copy(xT[:, 0:4, :], quarter(bank[0])).then_inc(x3T_ready, 1)
            act.wait_ge(gap_ready, 1)
            nc.scalar.activation(r1[:, 3:4], r1[:, 2:3], ACT.Exp).then_inc(gap_exp, 1)
            for k in range(0, KT, 2):
                act.wait_ge(gather_done, k + 1)
                nc.scalar.copy(xg_all[:, k, :, :], gather_bank(k)).then_inc(gather_read, 1)

            def unit(n):
                act.wait_ge(chunk_used, n * RING + W1C)
                nc.scalar.activation(h_s, ps_h[:, :], ACT.Relu).then_inc(h_ready, 1)
                act.wait_ge(chunk_used, n * RING + RING)
                nc.scalar.copy(y_s[:, 0:HALF], ps_y[0][:, :]).then_inc(y_ready, 1)

            act.wait_ge(table_ready, 1)
            jobs = act.value_load(table[0:1, 0:1], min_val=E, max_val=E + OVER)
            with act.Fori(0, jobs) as job:
                for u in range(UNITS):
                    unit(job * UNITS + u)
            act.wait_ge(scat_done, jobs * UNITS)
            nc.scalar.copy(out_s[:, 0:HALF], ps_o[0][0:N, :]).then_inc(out_ready, 1)

        @block.vector
        def _(dve):
            count = [0]

            def step(ins):
                count[0] += 1
                return ins.then_inc(dve_step, 1)

            def steps_done():
                dve.wait_ge(dve_step, count[0])

            tt, ts, stt = nc.vector.tensor_tensor, nc.vector.tensor_scalar, nc.vector.scalar_tensor_tensor

            def layernorm(n, src, done):
                for h in range(2):
                    step(nc.vector.bn_stats(stat[:, h, :], src[:, h * HALF:(h + 1) * HALF]))
                steps_done()
                nc.vector.bn_aggr(mv[:, :], stat[:, :, :].rearrange("p a b -> p (a b)")).then_inc(var_ready, 1)
                dve.wait_ge(std_ready, n)
                step(nc.vector.reciprocal(rstd[:, :], std[:, :]))
                steps_done()
                ts(xn[:, :], src[:, :], mv[:, 0:1], rstd[:, 0:1], ALU.subtract, ALU.mult).then_inc(done, 1)

            dve.wait_ge(x_in, 16)
            layernorm(1, x, xn_ready)

            dve.wait_ge(etw_in, 16)
            step(ts(sp[:, 3, :], etw[:, :], -1.0, None, ALU.mult))
            steps_done()
            step(tt(sp[:, 3, :], sp[:, 3, :], etw[:, :], ALU.max))
            steps_done()
            ts(sp[:, 0, :], sp[:, 3, :], -1.0, None, ALU.mult).then_inc(etw_abs, 1)
            dve.wait_ge(etw_abs, 1)
            step(ts(sp[:, 3, :], etw[:, :], 0.0, None, ALU.max))

            dve.wait_ge(rows_in, 16)
            nc.vector.tensor_copy(rows16, rows_i).then_inc(rows_ready, 1)
            dve.wait_ge(cols_in, 16)
            step(nc.vector.tensor_copy(cols[:, :, :], cols_i[:, :, :]))
            step(nc.vector.tensor_copy(cols16[:, :, :], cols_i[:, :, :]))
            dve.wait_ge(const_ready, 6)
            dve.wait_ge(rows_ready, 1)
            nc.vector.nop().then_inc(rows_read, 1)
            steps_done()
            cell, cls, code, dup, keep, t8 = (ec[:, i, :] for i in range(6))
            step(stt(cell, cols[:, 0, :], float(N), cols[:, 1, :], ALU.mult, ALU.add))
            step(ts(cls, cols[:, 2, :], 0.0, 4.0, ALU.is_equal, ALU.mult))
            step(nc.vector.tensor_copy(t8, code_i[:, :]))
            steps_done()
            step(tt(cls, cls, cols[:, 2, :], ALU.add))
            for g in range(NG):
                a, n = g * EG, min(EG, EC - g * EG)
                dve.wait_ge(cell_done, g + 1)
                ins = tt(same[:, a:a + n, :], edge_bank(bank[g % 2], n),
                         cell[:, a:a + n, None].to_broadcast([N, n, N]), ALU.is_equal)
                ins.then_inc(same_done, 1)
            for one_hot, end in ((dst1h, 1), (src1h, 0)):
                tt(one_hot, iota16[:, None, :].to_broadcast([N, EC, N]),
                   cols16[:, end, :, None].to_broadcast([N, EC, N]), ALU.is_equal).then_inc(onehot_ready, 1)
            dve.wait_ge(same_done, NG)
            step(tt(same, same, tri16[:, None, :].to_broadcast([N, EC, N]), ALU.mult))
            steps_done()
            step(nc.vector.tensor_reduce(dup, same, AX.X, ALU.max))
            step(tt(code, cls, t8, ALU.add))
            steps_done()
            step(ts(keep, dup, -1.0, 1.0, ALU.mult, ALU.add))
            steps_done()
            tt(kv16[:, :], code, keep, ALU.mult).then_inc(kv_ready, 1)
            dve.wait_ge(bo_in, 16)
            step(tt(x[:, :], x[:, :], x2[:, :], ALU.add))
            steps_done()
            dve.wait_ge(etw_ln, 1)
            step(tt(etw[:, :], sp[:, 3, :], sp[:, 2, :], ALU.add))
            for g in range(NG):
                n = min(EG, EC - g * EG)
                dve.wait_ge(map_done, g + 1)
                step(nc.vector.tensor_reduce(merged if g == 0 else mtmp,
                                             edge_bank(bank[(0, 1, 6, 7)[g % 4]], n).rearrange("p t j -> p j t"),
                                             AX.X, ALU.max))
                steps_done()
                if g:
                    step(tt(merged, merged, mtmp, ALU.max))
                    steps_done()
                nc.vector.nop().then_inc(map_read, 1)
            step(nc.vector.tensor_copy(mcode_i, merged))
            steps_done()
            step(nc.vector.tensor_single_scalar(mcode_i, mcode_i, SHIFT - 1, ALU.bitwise_and))
            steps_done()
            step(nc.vector.tensor_copy(merged, mcode_i))
            steps_done()
            step(stt(mtmp, merged, 0.0, ident[0:N, 0:N], ALU.is_equal, ALU.mult))
            steps_done()
            step(stt(merged, mtmp, 4.0, merged, ALU.mult, ALU.add))
            steps_done()
            step(ts(mask[:, :], merged, 0.0, FAR, ALU.is_equal, ALU.mult))
            for c in range(4):
                step(ts(mtmp, merged, float(c + 1), etw[:, c:c + 1], ALU.is_equal, ALU.mult))
                steps_done()
                step(tt(mask[:, :], mask[:, :], mtmp, ALU.add))
                steps_done()

            for b in range(4):
                s = attnv[:, 4 * b:4 * b + 4, :]
                dve.wait_ge(score_done, b + 1)
                step(stt(s, quarter(bank[(0, 1, 6, 7)[b]], N), SCALE, mask[:, None, :].to_broadcast([N, 4, N]),
                         ALU.mult, ALU.add))
                steps_done()
                step(nc.vector.tensor_reduce(smx[:, b, :], s, AX.X, ALU.max))
                steps_done()
                tt(s, s, smx[:, b, :, None].to_broadcast([N, 4, N]), ALU.subtract).then_inc(score_sub, 1)
            for b in range(4):
                s = attnv[:, 4 * b:4 * b + 4, :]
                dve.wait_ge(score_exp, b + 1)
                step(nc.vector.tensor_reduce(ssum[:, b, :], s, AX.X, ALU.add))
                steps_done()
                step(nc.vector.reciprocal(ssum[:, b, :], ssum[:, b, :]))
                steps_done()
                tt(s, s, ssum[:, b, :, None].to_broadcast([N, 4, N]), ALU.mult).then_inc(probs_ready, 1)
            dve.wait_ge(biv_in, 16)
            for h in range(2):
                dve.wait_ge(v2_done, h + 1)
                half = slice(h * HALF, (h + 1) * HALF)
                tt(v2[:, half], bank[2 + h][0:N, :], v2[:, half], ALU.add).then_inc(v2_ready, 1)

            for h in range(2):
                dve.wait_ge(o_done, h + 1)
                half = slice(h * HALF, (h + 1) * HALF)
                tt(x2[:, half], bank[2 + h][0:N, :], x[:, half], ALU.add).then_inc(x2_ready, 1)
            dve.wait_ge(x2_ready, 2)
            layernorm(2, x2, x3_ready)
            step(nc.vector.tensor_copy(kk[:, :, :], iota_f[:, 0:OVER, None].to_broadcast([N, OVER, E])))
            step(ts(rt[:, 15, :], iota_f[:, 0:E], -1.0, float(E), ALU.mult, ALU.add))
            dve.wait_ge(x3T_done, 2)
            nc.vector.tensor_copy(xT[:, 4:8, :], quarter(bank[1])).then_inc(x3T_ready, 1)

            lg, first, second, rest, pick, tmp, chosen, gates, rank1, spare, start, extra = (
                rt[:, i, :] for i in range(12))
            order = rt[:, 15, :]
            dve.wait_ge(logit_done, 1)
            step(nc.vector.tensor_copy(lg, bank[6][0:N, 0:E]))
            steps_done()

            def argmax(values, top, onehot):
                step(nc.vector.tensor_reduce(top, values, AX.X, ALU.max))
                steps_done()
                step(stt(tmp, values, top, order, ALU.is_equal, ALU.mult))
                steps_done()
                step(nc.vector.tensor_reduce(r1[:, 8:9], tmp, AX.X, ALU.max))
                steps_done()
                step(ts(onehot, order, r1[:, 8:9], None, ALU.is_equal))
                steps_done()

            argmax(lg, r1[:, 0:1], first)
            step(stt(rest, first, 2 * FAR, lg, ALU.mult, ALU.add))
            steps_done()
            argmax(rest, r1[:, 1:2], second)
            tt(r1[:, 2:3], r1[:, 1:2], r1[:, 0:1], ALU.subtract).then_inc(gap_ready, 1)
            tt(chosen, first, second, ALU.add).then_inc(chosen_ready, 1)
            dve.wait_ge(gap_exp, 1)
            step(ts(r1[:, 4:5], r1[:, 3:4], 1.0, None, ALU.add))
            steps_done()
            step(nc.vector.reciprocal(r1[:, 5:6], r1[:, 4:5]))
            steps_done()
            step(tt(r1[:, 6:7], r1[:, 5:6], r1[:, 3:4], ALU.mult))
            step(ts(tmp, first, r1[:, 5:6], None, ALU.mult))
            steps_done()
            step(stt(gates, second, r1[:, 6:7], tmp, ALU.mult, ALU.add))

            dve.wait_ge(rank_done, 1)
            dve.wait_ge(chosen_ready, 1)
            step(stt(rank1, bank[7][0:N, 0:E], 1.0, chosen, ALU.add, ALU.mult))
            step(ts(extra, bank[7][0:N, E:2 * E], float(SLOTS), None, ALU.is_gt))
            step(ts(spare, bank[7][0:N, E:2 * E], float(2 * SLOTS), None, ALU.is_gt))
            steps_done()
            step(tt(extra, extra, spare, ALU.add))
            step(ts(jp[:, 0:E], rank1, -1.0, None, ALU.add))
            step(nc.vector.tensor_copy(jg[:, 0:E], gates))
            step(nc.vector.memset(start[:, 0:1], 0.0))
            steps_done()
            for e in range(1, E):
                step(tt(start[:, e:e + 1], start[:, e - 1:e], extra[:, e - 1:e], ALU.add))
                steps_done()
            step(tt(spare, start, extra, ALU.add))
            wide = [N, OVER, E]
            own, ge, val, vg = (ov[:, i, :, :] for i in range(4))
            step(tt(ge, kk[:, :, :], start[:, None, :].to_broadcast(wide), ALU.is_ge))
            steps_done()
            step(tt(own, kk[:, :, :], spare[:, None, :].to_broadcast(wide), ALU.is_lt))
            steps_done()
            step(tt(own, own, ge, ALU.mult))
            step(tt(val, start[:, None, :].to_broadcast(wide), kk[:, :, :], ALU.subtract))
            steps_done()
            step(ts(val, val, float(SLOTS), -float(SLOTS), ALU.mult, ALU.add))
            steps_done()
            step(tt(val, val, rank1[:, None, :].to_broadcast(wide), ALU.add))
            steps_done()
            step(tt(val, val, own, ALU.mult))
            step(tt(vg, own, gates[:, None, :].to_broadcast(wide), ALU.mult))
            steps_done()
            step(nc.vector.tensor_reduce(ot[:, 0, :], val, AX.X, ALU.add))
            step(nc.vector.tensor_reduce(jg[:, E:E + OVER], vg, AX.X, ALU.add))
            step(nc.vector.memset(jp[:, E + OVER:], -1.0))
            step(nc.vector.memset(jg[:, E + OVER:], 0.0))
            steps_done()
            step(ts(jp[:, E:E + OVER], ot[:, 0, :], -1.0, None, ALU.add))
            steps_done()
            tt(sel, iota_f[:, None, 0:SLOTS].to_broadcast([N, JOBS, SLOTS]),
               jp[:, :, None].to_broadcast([N, JOBS, SLOTS]), ALU.is_equal).then_inc(sel_ready, 1)
            step(tt(tmp, iota_f[:, 0:E], iota_f[:, 0:E], ALU.bypass))
            step(nc.vector.tensor_copy(ge, iota_f[:, None, 0:E].to_broadcast(wide)))
            step(nc.vector.tensor_reduce(r1[:, 9:10], extra, AX.X, ALU.add))
            steps_done()
            step(tt(ge, ge, own, ALU.mult))
            steps_done()
            step(nc.vector.tensor_reduce(ot[:, 1, :], ge, AX.X, ALU.add))
            step(ts(r1[:, 10:11], r1[:, 9:10], float(E), None, ALU.add))
            steps_done()
            step(nc.vector.tensor_copy(table[0:1, 0:1], r1[0:1, 10:11]))
            step(nc.vector.tensor_copy(table[0:1, 1:1 + OVER], ot[0:1, 1, :]))
            steps_done()
            nc.vector.nop().then_inc(table_ready, 1)
            dve.wait_ge(table_ready, 1)
            for k in range(1, KT, 2):
                dve.wait_ge(gather_done, k + 1)
                nc.vector.tensor_copy(xg_all[:, k, :, :], gather_bank(k)).then_inc(gather_read, 1)
            dve.wait_ge(gather_read, KT)
            nc.vector.tensor_copy(xg, xg_all[:, :, 0, :]).then_inc(xg_ready, 1)
            dve.wait_ge(sel_ready, 1)
            step(tt(sel, sel, jg[:, :, None].to_broadcast([N, JOBS, SLOTS]), ALU.mult))
            steps_done()
            tt(selg, sel[:, :, None, :].to_broadcast([N, JOBS, 4, SLOTS]),
               sel[:, :, None, :].to_broadcast([N, JOBS, 4, SLOTS]), ALU.max).then_inc(selg_ready, 1)
            for q in range(0, JOBS, 4):
                n = min(4, JOBS - q)
                dve.wait_ge(sct_done, q // 4 + 1)
                nc.vector.tensor_copy(sc_all[:, q:q + n, :], quarter(bank[(6, 7)[q // 4 % 2]], P, n)).then_inc(sct_read, 1)
            dve.wait_ge(sct_read, -(-JOBS // 4))
            nc.vector.tensor_copy(sc, sc_all[:, 0, :]).then_inc(sc_ready, 1)

            def job_steps(job):
                for u in range(UNITS):
                    n = job * UNITS + u
                    dve.wait_ge(hT_done, n + 1)
                    nc.vector.tensor_copy(h_T, ps_t[:, :]).then_inc(hT_ready, 1)
                    if u == UNITS - 1:
                        nc.vector.tensor_copy(xg, xg_all[:, :, bass.ds(job + 1, 1), :]).then_inc(xg_ready, 1)
                    dve.wait_ge(chunk_used, n * RING + RING)
                    nc.vector.tensor_copy(y_s[:, HALF:D], ps_y[1][:, :]).then_inc(y_ready, 1)
                dve.wait_ge(scat_done, job * UNITS + UNITS)
                nc.vector.tensor_copy(sc, sc_all[:, bass.ds(job + 1, 1), :]).then_inc(sc_ready, 1)

            jobs = dve.value_load(table[0:1, 0:1], min_val=E, max_val=E + OVER)
            with dve.Fori(0, jobs) as job:
                job_steps(job)
            dve.wait_ge(scat_done, jobs * UNITS)
            nc.vector.tensor_copy(out_s[:, HALF:D], ps_o[1][0:N, :]).then_inc(out_ready, 1)

        @block.tensor
        def _(pe):
            mm = nc.tensor.matmul

            def chunk_tile(g, k):
                return slot(gslot(g)).rearrange("p (k n) -> p k n", k=KT)[:, k, :]

            def project_T(m, actT, out_banks):
                for h in range(2):
                    g = 2 * m + h
                    pe.wait_ge(gnn_in[g], 16)
                    for t in range(4):
                        for k in range(KT):
                            last = mm(bank[out_banks[h]][:, P * t:P * t + N], chunk_tile(g, k)[:, P * t:P * t + P],
                                      actT[:, k, :], start=(k == 0), stop=(k == KT - 1))
                    last.then_inc(gnn_used, 1)
                    yield h

            def project(m, actT, done):
                for h in range(2):
                    g = 2 * m + h
                    pe.wait_ge(gnn_in[g], 16)
                    for k in range(KT):
                        last = mm(bank[2 + h][0:N, :], actT[:, k, :], chunk_tile(g, k), start=(k == 0),
                                  stop=(k == KT - 1))
                    last.then_inc(done, 1)
                    pe.wait_ge(done, h + 1)
                    pe.nop().then_inc(gnn_used, 1)

            def transposes(src, dst_banks, rows_in, done):
                for b in range(2):
                    for t in range(4):
                        last = nc.tensor.transpose(bank[dst_banks[b]][:, P * t:P * t + rows_in],
                                                   src[:, P * (4 * b + t):P * (4 * b + t + 1)], ident[0:N, 0:N])
                    last.then_inc(done, 1)

            def map_groups(groups):
                for g in groups:
                    b = bank[(0, 1, 6, 7)[g % 4]]
                    if g >= 4:
                        pe.wait_ge(map_read, g - 3)
                    for t in range(g * EG, min(EC, g * EG + EG)):
                        c = (t - g * EG) * N
                        last = mm(b[0:N, c:c + N], src1h[:, t, :], dst1h[:, t, :], start=True, stop=True)
                    last.then_inc(map_done, 1)

            pe.wait_ge(const_ready, 6)
            pe.wait_ge(xn_ready, 1)
            transposes(xn, (0, 1), N, xT_done)
            pe.wait_ge(xT_ready, 2)
            pe.wait_ge(rows_ready, 1)
            for g in range(NG):
                a, n = g * EG, min(EG, EC - g * EG)
                if g >= 2:
                    pe.wait_ge(same_done, g - 1)
                mm(bank[g % 2][0:N, 0:n * N], pair16[:, :], rows16[:, a * N:(a + n) * N], start=True,
                   stop=True).then_inc(cell_done, 1)
            for _h in project_T(Q, xT, (2, 3)):
                pass
            pe.wait_ge(same_done, NG)
            for h in project_T(K, xT, (4, 5)):
                if h == 0:
                    pe.wait_ge(code_ready, 1)
                    pe.wait_ge(onehot_ready, 2)
                    map_groups(range(4))
                else:
                    map_groups(range(4, NG))
            pe.wait_ge(map_read, NG)
            pe.wait_ge(proj_read, 2)
            for _h in project_T(Q2, qvT, (6, 7)):
                pass
            for _h in project_T(V, xT, (2, 3)):
                pass
            pe.wait_ge(proj_read, 4)
            for _h in project_T(K2, koT, (4, 5)):
                pass
            pe.wait_ge(proj_read, 10)
            for b in range(4):
                for c in range(4):
                    h = 8 * (b // 2) + 2 * c + b % 2
                    r = slice(HD * (h % 2), HD * (h % 2) + HD)
                    last = mm(bank[(0, 1, 6, 7)[b]][0:N, P * c:P * c + N], q2Tv[r, h // 2, :], k2Tv[r, h // 2, :],
                              start=True, stop=True)
                last.then_inc(score_done, 1)
            project(V2, qvT, v2_done)
            for b in range(4):
                pe.wait_ge(probs_ready, b + 1)
                for c in range(4):
                    last = nc.tensor.transpose(bank[(0, 1, 6, 7)[b]][0:N, P * c:P * c + N], attnv[:, 4 * b + c, :],
                                               ident[0:N, 0:N])
                last.then_inc(probsT_done, 1)
            pe.wait_ge(v2_ready, 2)
            for half in range(2):
                for par in range(2):
                    b = 2 * half + par
                    pe.wait_ge(probsT_ready, b + 1)
                    for c in range(4):
                        h = 8 * half + 2 * c + par
                        last = mm(bank[4 + half][HD * par:HD * par + HD, P * c:P * c + N],
                                  v2[:, HD * h:HD * h + HD], attnTv[:, 4 * b + c, :], start=True, stop=True)
                last.then_inc(pv_done, 1)
            pe.wait_ge(oT_ready, 2)
            project(O, koT, o_done)
            pe.wait_ge(x2_ready, 2)
            for h in range(2):
                mm(ps_o[h][0:N, :], ident[0:N, 0:N], x2[:, h * HALF:(h + 1) * HALF], start=True, stop=False,
                   skip_group_check=True)
            pe.wait_ge(x3_ready, 1)
            transposes(xn, (0, 1), N, x3T_done)
            pe.wait_ge(x3T_ready, 2)
            pe.wait_ge(gate_in, 16)
            for k in range(KT):
                last = mm(bank[6][0:N, 0:E], xT[:, k, :], gate_w[:, k, :], start=(k == 0), stop=(k == KT - 1))
            last.then_inc(logit_done, 1)
            pe.wait_ge(chosen_ready, 1)
            mm(bank[7][0:N, 0:E], upper[:, :], rt[:, 6, :], start=True, stop=True)
            mm(bank[7][0:N, E:2 * E], ones[:, :], rt[:, 6, :], start=True, stop=True).then_inc(rank_done, 1)
            pe.wait_ge(sel_ready, 1)
            for k in range(KT):
                if k >= 4:
                    pe.wait_ge(gather_read, k)
                mm(bank[(0, 1, 6, 7)[k % 4]][:, 0:JOBS * SLOTS], xn[:, k * P:(k + 1) * P],
                   sel.rearrange("p j s -> p (j s)"), start=True, stop=True).then_inc(gather_done, 1)
            pe.wait_ge(gather_read, KT)
            pe.wait_ge(selg_ready, 1)
            for q in range(0, JOBS, 4):
                if q >= 8:
                    pe.wait_ge(sct_read, q // 4 - 1)
                for j in range(q, min(JOBS, q + 4)):
                    last = mm(bank[(6, 7)[q // 4 % 2]][:, P * (j - q):P * (j - q) + N],
                              selg[:, j, :, :].rearrange("p c s -> p (c s)"), ident[0:N, 0:N], start=True, stop=True)
                last.then_inc(sct_done, 1)

            def job_products(job):
                for u in range(UNITS):
                    n = job * UNITS + u
                    landed = n * 16 + 16
                    if u == 0:
                        pe.wait_ge(xg_ready, job + 1)
                    for c in range(W1C):
                        pe.wait_ge(ring_in[c], landed)
                        w = slot(c).rearrange("p (k f) -> p k f", f=UF)
                        ks = KT // W1C
                        for k in range(ks):
                            for j in range(4):
                                last = mm(ps_h[SLOTS * j:SLOTS * (j + 1), :], xg[:, ks * c + k, :],
                                          w[:, k, HALF * j:HALF * (j + 1)], start=(c == 0 and k == 0),
                                          stop=(c == W1C - 1 and k == ks - 1))
                        last.then_inc(chunk_used, 1)
                    pe.wait_ge(h_ready, n + 1)
                    for c in range(CT):
                        last = nc.tensor.transpose(ps_t[:, P * c:P * c + P], h_s[:, P * c:P * c + P], ident[:, :])
                    last.then_inc(hT_done, 1)
                    pe.wait_ge(hT_ready, n + 1)
                    for c in range(W2C):
                        pe.wait_ge(ring_in[W1C + c], landed)
                        w = slot(W1C + c).rearrange("p (j d) -> p j d", d=D)
                        for d in range(2):
                            for j in range(4):
                                last = mm(ps_y[d][SLOTS * j:SLOTS * (j + 1), :],
                                          h_T[:, P * c + SLOTS * j:P * c + SLOTS * (j + 1)],
                                          w[:, j, HALF * d:HALF * (d + 1)], start=(c == 0), stop=(c == W2C - 1))
                        last.then_inc(chunk_used, 1)
                    pe.wait_ge(y_ready, n * 2 + 2)
                    if u == 0:
                        pe.wait_ge(sc_ready, job + 1)
                    for d in range(2):
                        last = mm(ps_o[d][0:N, :], sc, y_s[:, HALF * d:HALF * (d + 1)], start=False, stop=False,
                                  skip_group_check=True)
                    last.then_inc(scat_done, 1)

            pe.wait_ge(table_ready, 1)
            jobs = pe.value_load(table[0:1, 0:1], min_val=E, max_val=E + OVER)
            with pe.Fori(0, jobs) as job:
                job_products(job)


def _col_layout(w):
    return w.T.reshape(KT, P, 2, HALF).transpose(2, 1, 0, 3).reshape(2, P, CHUNK)


def _layout(a):
    w = {k: np.asarray(v) for k, v in a.items()}
    g = {k[7:]: v for k, v in w.items() if k.startswith("L0_gnn_")}
    gnn = np.concatenate([_col_layout(g[k]) for k in ("wq", "wk", "wiq", "wv", "wik", "wiv", "wo")])
    colb = np.stack([g[k] for k in ("bq", "bk", "biq", "bv", "bik")]).reshape(5, KT, P).transpose(2, 0, 1)
    edges = np.stack([w["src"], w["dst"], w["edge_type_5"]])
    w1 = w["L0_ffn_w1"].reshape(E, UNITS, UF, W1C, KT // W1C, P).transpose(0, 1, 3, 5, 4, 2)
    w2 = w["L0_ffn_w2"].reshape(E, D, UNITS, 4, CT, P).transpose(0, 2, 4, 5, 3, 1)
    return {
        "x": w["x"],
        "rows": edges[0:2],
        "cols": edges.reshape(3, EC, N).transpose(2, 0, 1),
        "etw": g["edge_type_weights"].reshape(1, 4),
        "gnn_w": gnn,
        "colb": colb,
        "biv": g["biv"].reshape(1, D),
        "bo": g["bo"].reshape(1, D),
        "gate": w["L0_ffn_gate_w"].T.reshape(KT, P, E).transpose(1, 0, 2),
        "w1": w1.reshape(E, UNITS, W1C, P, CHUNK),
        "w2": w2.reshape(E, UNITS, W2C, P, CHUNK),
    }


def kernel(**inputs):
    import concourse.bacc as bacc
    from concourse.bass_utils import run_bass_kernel_spmd

    nc = bacc.Bacc("TRN2", target_bir_lowering=False, num_devices=1)
    arrays, args = {}, []
    for name, a in _layout(inputs).items():
        a = np.ascontiguousarray(a)
        arrays[f"in_{name}"] = a
        args.append(nc.dram_tensor(f"in_{name}", a.shape, mybir.dt.from_np(a.dtype), kind="ExternalInput").ap())
    out = nc.dram_tensor("out_0", (N, D), F32, kind="ExternalOutput").ap()
    gnn_moe_kernel(nc, *args, out)
    r = run_bass_kernel_spmd(nc, [arrays], core_ids=[0])
    return r.results[0]["out_0"]
```

```python
from contextlib import ExitStack

import numpy as np

import concourse.bass as bass
from concourse import mybir

F32 = mybir.dt.float32
F16 = mybir.dt.float16
I32 = mybir.dt.int32
ALU = mybir.AluOpType
ACT = mybir.ActivationFunctionType
AX = mybir.AxisListType

P = 128
N = 96
D = 1024
KT = D // P
HEADS = 16
HD = D // HEADS
E = 8
F = 4 * D
EDGES = 3168
EC = EDGES // N
EG = 5
NG = -(-EC // EG)
HALF = 512
SLOTS = 32
OVER = (2 * N) // (SLOTS + 1)
JOBS = E + OVER + 1
UNITS = 2
UF = F // UNITS
CT = UF // P // 4
CHUNK = 2048
W1C = KT * UF // CHUNK
W2C = (UF // P) * D // CHUNK
RING = 16
EXTRA = 4
SLOTS_ALL = RING + EXTRA
PER_JOB = UNITS * (W1C + W2C)
AGAIN = PER_JOB - SLOTS_ALL
EPS = 1e-5
FAR = -1e30
SCALE = 1.0 / 8.0
SHIFT = 8
assert EC * N == EDGES and W1C + W2C == RING and HD * HEADS == D and SCALE * SCALE * HD == 1.0
assert UF == 4 * HALF and CT * 4 * P == UF and W1C == KT and W2C == 2 * CT and 0 < AGAIN <= RING

Q, K, Q2, K2, V, V2, O = range(7)
GC = 4
CW = D // GC
NGC = 7 * GC


def gslot(g):
    return (g - (NGC - SLOTS_ALL)) % SLOTS_ALL


def first_slot(c):
    return c % SLOTS_ALL


def gnn_moe_kernel(nc, x_d, rows_d, cols_d, etw_d, gnn_w_d, colb_d, biv_d, bo_d, gate_d, w1_d, w2_d, out_d):
    with ExitStack() as ctx:
        def sb(name, shape, dt=F32):
            return ctx.enter_context(nc.sbuf_tensor(name, shape, dt))

        def sem(name):
            return ctx.enter_context(nc.semaphore(name))

        ring = sb("ring", [P, SLOTS_ALL * CHUNK])

        def slot(s, n=1):
            return ring[:, s * CHUNK:(s + n) * CHUNK]

        rows_i = slot(6, 2)[0:2, 0:EDGES].bitcast(I32)
        early = slot(8, 4).bitcast(F16)
        rows16 = early[0:2, 0:EDGES]
        same = early[0:N, EDGES:2 * EDGES].rearrange("p (t j) -> p t j", j=N)
        src1h = early[0:N, 2 * EDGES:3 * EDGES].rearrange("p (t j) -> p t j", j=N)
        dst1h = early[0:N, 3 * EDGES:4 * EDGES].rearrange("p (t j) -> p t j", j=N)
        x = sb("x", [N, D])
        xn = sb("xn", [N, D])
        x2 = sb("x2", [N, D])
        xT = sb("xT", [P, KT, N])
        qvT = sb("qvT", [P, KT, N])
        koT = sb("koT", [P, KT, N])
        qk2T = sb("qk2T", [P, 2 * KT * N])
        q2Tv = qk2T[:, 0:KT * N].rearrange("p (k n) -> p k n", n=N)
        k2Tv = qk2T[:, KT * N:].rearrange("p (k n) -> p k n", n=N)
        v2 = qk2T[0:N, 0:D]
        attn = sb("attn", [P, HEADS * N])
        attnT = sb("attnT", [P, HEADS * N])
        attnv = attn[0:N, :].rearrange("p (h m) -> p h m", m=N)
        attnTv = attnT[0:N, :].rearrange("p (h m) -> p h m", m=N)
        h_s = qvT[:, :, :].rearrange("p k n -> p (k n)")[:, 0:HALF]
        h_T = koT[:, :, :].rearrange("p k n -> p (k n)")[:, 0:HALF]
        y_s = attn[:, 0:D]
        out_s = attnT[0:N, 0:D]
        xg = attn[:, D:D + 256].rearrange("p (k s) -> p k s", s=SLOTS)
        ov = attn[0:N, D + 256:D + 256 + 4 * OVER * E].rearrange("p (i k e) -> p i k e", i=4, e=E)
        pair = attnT[0:N, D:D + 2 * E * E].rearrange("p (i e f) -> p i e f", i=2, f=E)
        sel = attnT[0:N, D + 256:D + 256 + N]
        selg = attnT[0:N, D + 384:D + 512].rearrange("p (c s) -> p c s", s=SLOTS)

        ident = sb("ident", [P, P])
        upper = sb("upper", [N, N])
        ones = sb("ones", [N, N])
        tri16 = sb("tri16", [N, N], F16)
        iota_i = sb("iota_i", [N, N], I32)
        iota_f = sb("iota_f", [N, N])
        iota16 = sb("iota16", [N, N], F16)
        code_i = sb("code_i", [N, EC], I32)
        pair16 = sb("pair16", [2, N], F16)
        cols_i = sb("cols_i", [N, 3, EC], I32)
        cols = sb("cols", [N, 3, EC])
        cols16 = sb("cols16", [N, 3, EC], F16)
        ec = sb("ec", [N, 6, EC])
        kv16 = sb("kv16", [N, EC], F16)
        merged, mtmp = attnT[0:N, 0:N], attnT[0:N, N:2 * N]
        mcode_i = attnT[0:N, 2 * N:3 * N].bitcast(I32)
        mask = sb("mask", [N, N])
        etw = sb("etw", [N, 4])
        sp = sb("sp", [N, 4, 4])
        colb = sb("colb", [P, 5, KT])
        gate_w = sb("gate_w", [P, KT, E])
        stat = sb("stat", [N, 2, 6])
        mv = sb("mv", [N, 2])
        std = sb("std", [N, 1])
        rstd = sb("rstd", [N, 1])
        smx = sb("smx", [N, 4, 4])
        ssum = sb("ssum", [N, 4, 4])
        warm = sb("warm", [1, 1])
        rt = sb("rt", [N, 16, E])
        r1 = sb("r1", [N, 16])
        kk = sb("kk", [N, OVER, E])
        sc = sb("sc", [P, N])
        lower_i = sb("lower_i", [N, E, E], I32)
        jp = sb("jp", [N, JOBS])
        jg = sb("jg", [N, JOBS])
        ot = sb("ot", [N, 3, OVER])
        table = sb("table", [1, 1 + OVER], I32)

        bank = [ctx.enter_context(nc.psum_tensor(f"bank{b}", [P, HALF], F32)) for b in range(8)]
        ps_h, ps_t, ps_y, ps_o = bank[0], bank[1], bank[2:4], bank[4:6]

        def quarter(b, rows=P, n=4):
            return b[0:rows, :].rearrange("p (q c) -> p q c", c=P)[:, 0:n, 0:N]

        def edge_bank(b, t):
            return b[0:N, 0:t * N].rearrange("p (t j) -> p t j", j=N)

        gather_at = [(6, N * k) if k < 5 else (7, N * (k - 5)) for k in range(KT)]

        def gathered(b, n):
            return bank[b][:, 0:n * N].rearrange("p (k c) -> p k c", c=N)[:, :, 0:SLOTS]

        ps_sc = bank[7][:, 384:384 + N]
        assert 3 * N <= 384 and 5 * N <= HALF

        x_in, rows_in, cols_in, etw_in, colb_in, gate_in, biv_in, bo_in = (
            sem(s) for s in ("x_in", "rows_in", "cols_in", "etw_in", "colb_in", "gate_in", "biv_in", "bo_in"))
        gnn_in = [sem(f"gnn_in{g}") for g in range(NGC)]
        ring_in = [sem(f"ring_in{s}") for s in range(SLOTS_ALL)]
        gnn_used = sem("gnn_used")
        chunk_used = sem("chunk_used")
        const_ready = sem("const_ready")
        pool_step = sem("pool_step")
        dve_step = sem("dve_step")
        act_step = sem("act_step")
        rows_read = sem("rows_read")
        var_ready, std_ready = sem("var_ready"), sem("std_ready")
        xn_ready, xT_done, xT_ready = sem("xn_ready"), sem("xT_done"), sem("xT_ready")
        rows_ready = sem("rows_ready")
        cell_done, same_done = sem("cell_done"), sem("same_done")
        code_ready = sem("code_ready")
        map_done, map_read = sem("map_done"), sem("map_read")
        etw_exp, etw_ln = sem("etw_exp"), sem("etw_ln")
        etw_abs = sem("etw_abs")
        proj_read = sem("proj_read")
        score_done, score_sub, score_exp = sem("score_done"), sem("score_sub"), sem("score_exp")
        probs_ready, probsT_done, probsT_ready = sem("probs_ready"), sem("probsT_done"), sem("probsT_ready")
        v2_done, v2_ready = sem("v2_done"), sem("v2_ready")
        pv_done, oT_ready = sem("pv_done"), sem("oT_ready")
        o_done, x2_ready = sem("o_done"), sem("x2_ready")
        x3_ready, x3T_done, x3T_ready = sem("x3_ready"), sem("x3T_done"), sem("x3T_ready")
        logit_done, gap_ready, gap_exp = sem("logit_done"), sem("gap_ready"), sem("gap_exp")
        warm_ready = sem("warm_ready")
        chosen_ready, rank_done = sem("chosen_ready"), sem("rank_done")
        sel_ready, selg_ready = sem("sel_ready"), sem("selg_ready")
        gather_done, sct_done = sem("gather_done"), sem("sct_done")
        table_ready = sem("table_ready")
        xg_ready, sc_ready = sem("xg_ready"), sem("sc_ready")
        h_ready, hT_done, hT_ready = sem("h_ready"), sem("hT_done"), sem("hT_ready")
        y_ready = [sem("y_ready0"), sem("y_ready1")]
        scat_done = [sem("scat_done0"), sem("scat_done1")]
        out_ready = [sem("out_ready0"), sem("out_ready1")]
        stored = sem("stored")

        block = ctx.enter_context(nc.Block())

        @block.sync
        def _(sp_):
            sp_.dma_start(x[:, :], x_d).then_inc(x_in, 16)
            for g in range(NGC):
                if gslot(g) == 6:
                    sp_.wait_ge(rows_read, 1)
                if gslot(g) == 8:
                    sp_.wait_ge(map_done, NG)
                if g >= SLOTS_ALL:
                    sp_.wait_ge(gnn_used, g - SLOTS_ALL + 1)
                sp_.dma_start(slot(gslot(g)), gnn_w_d[g]).then_inc(gnn_in[g], 16)

            def expert_chunk(expert, c, s):
                u, r = c // RING, c % RING
                src = w1_d[expert, u, r] if r < W1C else w2_d[expert, u, r - W1C]
                sp_.dma_start(slot(s), src).then_inc(ring_in[s], 16)

            for c in range(PER_JOB):
                if c < SLOTS_ALL:
                    sp_.wait_ge(gnn_used, NGC - SLOTS_ALL + c + 1)
                else:
                    sp_.wait_ge(chunk_used, c - SLOTS_ALL + 1)
                expert_chunk(0, c, first_slot(c))
            for c in range(PER_JOB):
                before = SLOTS_ALL + c if c < AGAIN else c if c < RING else PER_JOB + c - RING
                sp_.wait_ge(chunk_used, before + 1)
                expert_chunk(1, c, c % RING)
            with sp_.Fori(2, E) as e:
                for c in range(PER_JOB):
                    sp_.wait_ge(chunk_used, e * PER_JOB + (c - RING + 1))
                    expert_chunk(e, c, c % RING)
            sp_.wait_ge(table_ready, 1)
            jobs = sp_.value_load(table[0:1, 0:1], min_val=E, max_val=E + OVER)
            with sp_.If(jobs > E):
                with sp_.Fori(E, jobs) as job:
                    e = sp_.value_load(table[0:1, bass.ds(job - (E - 1), 1)], min_val=0, max_val=E - 1)
                    for c in range(PER_JOB):
                        sp_.wait_ge(chunk_used, job * PER_JOB + (c - RING + 1))
                        expert_chunk(e, c, c % RING)
            for d in range(2):
                sp_.wait_ge(out_ready[d], 1)
                sp_.dma_start(out_d[:, HALF * d:HALF * (d + 1)], out_s[:, HALF * d:HALF * (d + 1)]).then_inc(stored, 16)
            sp_.wait_ge(stored, 32)

        @block.gpsimd
        def _(pool):
            pool.dma_start(cols_i[:, :, :], cols_d).then_inc(cols_in, 16)
            pool.memset(ones[:, :], 1.0).then_inc(pool_step, 1)
            pool.memset(ident[:, :], 1.0).then_inc(pool_step, 1)
            pool.memset(pair16[:, :], 1.0).then_inc(pool_step, 1)
            pool.iota(iota_i[:, :], [[1, N]], base=0, channel_multiplier=0).then_inc(pool_step, 1)
            pool.iota(code_i[:, :], [[SHIFT, EC]], base=0, channel_multiplier=0).then_inc(pool_step, 1)
            pool.wait_ge(pool_step, 5)
            pool.affine_select(out=ident[:, :], in_=ident[:, :], compare_op=ALU.is_equal, fill=0.0, base=0,
                               pattern=[[1, P]], channel_multiplier=-1).then_inc(const_ready, 1)
            pool.affine_select(out=upper[:, :], in_=ones[:, :], compare_op=ALU.is_gt, fill=0.0, base=0,
                               pattern=[[1, N]], channel_multiplier=-1).then_inc(const_ready, 1)
            pool.memset(pair16[0:1, :], float(N)).then_inc(const_ready, 1)
            pool.tensor_copy(iota_f[:, :], iota_i[:, :]).then_inc(const_ready, 1)
            pool.tensor_copy(iota16[:, :], iota_i[:, :]).then_inc(const_ready, 1)
            pool.wait_ge(const_ready, 5)
            pool.tensor_copy(tri16[:, :], upper[:, :]).then_inc(const_ready, 1)
            pool.iota(lower_i[:, :, :], [[1, E], [-1, E]], base=0, channel_multiplier=0).then_inc(const_ready, 1)

        @block.scalar
        def _(act):
            act.dma_start(rows_i, rows_d).then_inc(rows_in, 16)
            act.dma_start(etw[:, :], etw_d.to_broadcast([N, 4])).then_inc(etw_in, 16)
            act.dma_start(colb[:, :, :], colb_d).then_inc(colb_in, 16)
            act.dma_start(gate_w[:, :, :], gate_d).then_inc(gate_in, 16)
            act.dma_start(x2[:, :], bo_d.to_broadcast([N, D])).then_inc(bo_in, 16)
            def root(n):
                act.wait_ge(var_ready, n)
                nc.scalar.activation(std[:, :], mv[:, 1:2], ACT.Sqrt, bias=EPS).then_inc(std_ready, 1)

            act.wait_ge(warm_ready, 1)
            nc.scalar.activation(warm[:, :], warm[:, :], ACT.Sqrt).then_inc(act_step, 1)
            root(1)
            for b in range(2):
                act.wait_ge(xT_done, b + 1)
                nc.scalar.copy(xT[:, 4 * b:4 * b + 4, :], quarter(bank[b])).then_inc(xT_ready, 1)
            act.dma_start(xn[:, :], biv_d.to_broadcast([N, D])).then_inc(biv_in, 16)
            act.wait_ge(etw_abs, 1)
            nc.scalar.activation(sp[:, 1, :], sp[:, 0, :], ACT.Exp).then_inc(etw_exp, 1)
            act.wait_ge(etw_exp, 1)
            nc.scalar.activation(sp[:, 2, :], sp[:, 1, :], ACT.Ln, bias=1.0).then_inc(etw_ln, 1)
            act.wait_ge(colb_in, 16)
            banks = {Q: (2, 3), K: (4, 5), Q2: (6, 7), K2: (2, 3), V: (4, 5)}
            outs = {Q: qvT, K: koT, Q2: q2Tv, V: qvT, K2: k2Tv}
            for m in (Q, K, Q2, K2, V):
                for h in range(2):
                    act.wait_ge(gnn_used, GC * m + 2 * h + 2)
                    for t in range(4 * h, 4 * h + 4):
                        c = P * (t % 4)
                        last = nc.scalar.activation(outs[m][:, t, :], bank[banks[m][t // 4]][:, c:c + N],
                                                    ACT.Identity, bias=colb[:, m, t:t + 1])
                    last.then_inc(proj_read, 1)
            for b in range(4):
                act.wait_ge(score_sub, b + 1)
                s = attnv[:, 4 * b:4 * b + 4, :]
                nc.scalar.activation(s, s, ACT.Exp).then_inc(score_exp, 1)
            for b in range(4):
                act.wait_ge(probsT_done, b + 1)
                nc.scalar.copy(attnTv[:, 4 * b:4 * b + 4, :], quarter(bank[(0, 1, 6, 7)[b]], N)).then_inc(probsT_ready, 1)
            for b in range(2):
                act.wait_ge(pv_done, b + 1)
                nc.scalar.copy(koT[:, 4 * b:4 * b + 4, :], quarter(bank[4 + b])).then_inc(oT_ready, 1)
            nc.scalar.activation(warm[:, :], warm[:, :], ACT.Sqrt).then_inc(act_step, 1)
            root(2)
            act.wait_ge(x3T_done, 1)
            nc.scalar.copy(xT[:, 0:4, :], quarter(bank[0])).then_inc(x3T_ready, 1)
            act.wait_ge(gap_ready, 1)
            nc.scalar.activation(r1[:, 3:4], r1[:, 2:3], ACT.Exp).then_inc(gap_exp, 1)
            act.wait_ge(gather_done, 1)
            nc.scalar.copy(xg[:, 0:5, :], gathered(6, 5)).then_inc(xg_ready, 1)
            act.wait_ge(table_ready, 1)
            jobs = act.value_load(table[0:1, 0:1], min_val=E, max_val=E + OVER)
            with act.Fori(0, jobs) as job:
                for u in range(UNITS):
                    n = job * UNITS + u
                    act.wait_ge(chunk_used, n * RING + W1C)
                    nc.scalar.activation(h_s, ps_h[:, :], ACT.Relu).then_inc(h_ready, 1)
                    if u == UNITS - 1:
                        act.wait_ge(gather_done, job + 2)
                        nc.scalar.copy(xg[:, 0:5, :], gathered(6, 5)).then_inc(xg_ready, 1)
                    act.wait_ge(chunk_used, n * RING + W1C + CT)
                    nc.scalar.copy(y_s[:, 0:HALF], ps_y[0][:, :]).then_inc(y_ready[0], 1)
            act.wait_ge(scat_done[0], jobs * UNITS)
            nc.scalar.copy(out_s[:, 0:HALF], ps_o[0][0:N, :]).then_inc(out_ready[0], 1)

        @block.vector
        def _(dve):
            count = [0]

            def step(ins):
                count[0] += 1
                return ins.then_inc(dve_step, 1)

            def steps_done():
                dve.wait_ge(dve_step, count[0])

            tt, ts, stt = nc.vector.tensor_tensor, nc.vector.tensor_scalar, nc.vector.scalar_tensor_tensor

            def half_stats(src, h):
                step(nc.vector.bn_stats(stat[:, h, :], src[:, h * HALF:(h + 1) * HALF]))

            def layernorm(n, src, done):
                steps_done()
                nc.vector.bn_aggr(mv[:, :], stat[:, :, :].rearrange("p a b -> p (a b)")).then_inc(var_ready, 1)
                dve.wait_ge(std_ready, n)
                step(nc.vector.reciprocal(rstd[:, :], std[:, :]))
                steps_done()
                for h in range(2):
                    half = slice(h * HALF, (h + 1) * HALF)
                    ts(xn[:, half], src[:, half], mv[:, 0:1], rstd[:, 0:1], ALU.subtract, ALU.mult).then_inc(done, 1)

            nc.vector.memset(warm[:, :], 1.0).then_inc(warm_ready, 1)
            dve.wait_ge(x_in, 16)
            half_stats(x, 0)
            half_stats(x, 1)
            layernorm(1, x, xn_ready)

            dve.wait_ge(etw_in, 16)
            step(ts(sp[:, 3, :], etw[:, :], -1.0, None, ALU.mult))
            steps_done()
            step(tt(sp[:, 3, :], sp[:, 3, :], etw[:, :], ALU.max))
            steps_done()
            ts(sp[:, 0, :], sp[:, 3, :], -1.0, None, ALU.mult).then_inc(etw_abs, 1)
            dve.wait_ge(etw_abs, 1)
            step(ts(sp[:, 3, :], etw[:, :], 0.0, None, ALU.max))

            dve.wait_ge(rows_in, 16)
            nc.vector.tensor_copy(rows16, rows_i).then_inc(rows_ready, 1)
            dve.wait_ge(cols_in, 16)
            step(nc.vector.tensor_copy(cols[:, :, :], cols_i[:, :, :]))
            step(nc.vector.tensor_copy(cols16[:, :, :], cols_i[:, :, :]))
            dve.wait_ge(const_ready, 7)
            dve.wait_ge(rows_ready, 1)
            nc.vector.nop().then_inc(rows_read, 1)
            steps_done()
            cell, cls, code, dup, keep, t8 = (ec[:, i, :] for i in range(6))
            step(stt(cell, cols[:, 0, :], float(N), cols[:, 1, :], ALU.mult, ALU.add))
            step(ts(cls, cols[:, 2, :], 0.0, 4.0, ALU.is_equal, ALU.mult))
            step(nc.vector.tensor_copy(t8, code_i[:, :]))
            steps_done()
            step(tt(cls, cls, cols[:, 2, :], ALU.add))
            for one_hot, end in ((dst1h, 1), (src1h, 0)):
                step(tt(one_hot, iota16[:, None, :].to_broadcast([N, EC, N]),
                        cols16[:, end, :, None].to_broadcast([N, EC, N]), ALU.is_equal))
            for g in range(NG):
                a, n = g * EG, min(EG, EC - g * EG)
                dve.wait_ge(cell_done, g + 1)
                ins = tt(same[:, a:a + n, :], edge_bank(bank[g % 2], n),
                         cell[:, a:a + n, None].to_broadcast([N, n, N]), ALU.is_equal)
                ins.then_inc(same_done, 1)
            dve.wait_ge(same_done, NG)
            step(tt(same, same, tri16[:, None, :].to_broadcast([N, EC, N]), ALU.mult))
            steps_done()
            step(nc.vector.tensor_reduce(dup, same, AX.X, ALU.max))
            step(tt(code, cls, t8, ALU.add))
            steps_done()
            step(ts(keep, dup, -1.0, 1.0, ALU.mult, ALU.add))
            steps_done()
            step(tt(kv16[:, :], code, keep, ALU.mult))
            steps_done()
            tt(dst1h, dst1h, kv16[:, :, None].to_broadcast([N, EC, N]), ALU.mult).then_inc(code_ready, 1)
            dve.wait_ge(bo_in, 16)
            step(tt(x[:, :], x[:, :], x2[:, :], ALU.add))
            steps_done()
            dve.wait_ge(etw_ln, 1)
            step(tt(etw[:, :], sp[:, 3, :], sp[:, 2, :], ALU.add))
            for g in range(NG):
                n = min(EG, EC - g * EG)
                dve.wait_ge(map_done, g + 1)
                step(nc.vector.tensor_reduce(merged if g == 0 else mtmp,
                                             edge_bank(bank[g % 4], n).rearrange("p t j -> p j t"),
                                             AX.X, ALU.max))
                steps_done()
                if g:
                    step(tt(merged, merged, mtmp, ALU.max))
                    steps_done()
                nc.vector.nop().then_inc(map_read, 1)
            step(nc.vector.tensor_copy(mcode_i, merged))
            steps_done()
            step(nc.vector.tensor_single_scalar(mcode_i, mcode_i, SHIFT - 1, ALU.bitwise_and))
            steps_done()
            step(nc.vector.tensor_copy(merged, mcode_i))
            steps_done()
            step(stt(mtmp, merged, 0.0, ident[0:N, 0:N], ALU.is_equal, ALU.mult))
            steps_done()
            step(stt(merged, mtmp, 4.0, merged, ALU.mult, ALU.add))
            steps_done()
            step(ts(mask[:, :], merged, 0.0, FAR, ALU.is_equal, ALU.mult))
            for c in range(4):
                step(ts(mtmp, merged, float(c + 1), etw[:, c:c + 1], ALU.is_equal, ALU.mult))
                steps_done()
                step(tt(mask[:, :], mask[:, :], mtmp, ALU.add))
                steps_done()

            for b in range(4):
                s = attnv[:, 4 * b:4 * b + 4, :]
                dve.wait_ge(score_done, b + 1)
                step(stt(s, quarter(bank[(0, 1, 6, 7)[b]], N), SCALE, mask[:, None, :].to_broadcast([N, 4, N]),
                         ALU.mult, ALU.add))
                steps_done()
                step(nc.vector.tensor_reduce(smx[:, b, :], s, AX.X, ALU.max))
                steps_done()
                tt(s, s, smx[:, b, :, None].to_broadcast([N, 4, N]), ALU.subtract).then_inc(score_sub, 1)
            for b in range(4):
                s = attnv[:, 4 * b:4 * b + 4, :]
                dve.wait_ge(score_exp, b + 1)
                step(nc.vector.tensor_reduce(ssum[:, b, :], s, AX.X, ALU.add))
                steps_done()
                step(nc.vector.reciprocal(ssum[:, b, :], ssum[:, b, :]))
                steps_done()
                tt(s, s, ssum[:, b, :, None].to_broadcast([N, 4, N]), ALU.mult).then_inc(probs_ready, 1)
            dve.wait_ge(biv_in, 16)
            for h in range(2):
                dve.wait_ge(v2_done, 2 * h + 2)
                half = slice(h * HALF, (h + 1) * HALF)
                tt(v2[:, half], bank[2 + h][0:N, :], xn[:, half], ALU.add).then_inc(v2_ready, 1)

            step(nc.vector.tensor_copy(kk[:, :, :], iota_f[:, 0:OVER, None].to_broadcast([N, OVER, E])))
            step(nc.vector.tensor_single_scalar(lower_i[:, :, :], lower_i[:, :, :], 0, ALU.is_gt))
            step(nc.vector.memset(rt[:, 10, 0:1], 0.0))
            for h in range(2):
                dve.wait_ge(o_done, 2 * h + 2)
                half = slice(h * HALF, (h + 1) * HALF)
                tt(x2[:, half], bank[2 + h][0:N, :], x[:, half], ALU.add).then_inc(x2_ready, 1)
                dve.wait_ge(x2_ready, h + 1)
                half_stats(x2, h)
            dve.wait_ge(v2_ready, 2)
            layernorm(2, x2, x3_ready)
            dve.wait_ge(x3T_done, 2)
            nc.vector.tensor_copy(xT[:, 4:8, :], quarter(bank[1])).then_inc(x3T_ready, 1)

            lg, first, second, standing, tmp, rank1, chosen, gates, spare, extra, start, second_l = (
                rt[:, i, :] for i in range(12))
            dve.wait_ge(logit_done, 1)
            step(nc.vector.tensor_copy(lg, bank[6][0:N, 0:E]))
            steps_done()
            square = [N, E, E]
            step(tt(pair[:, 0, :, :], lg[:, None, :].to_broadcast(square), lg[:, :, None].to_broadcast(square),
                    ALU.is_gt))
            step(tt(pair[:, 1, :, :], lg[:, None, :].to_broadcast(square), lg[:, :, None].to_broadcast(square),
                    ALU.is_ge))
            steps_done()
            step(nc.vector.copy_predicated(pair[:, 0, :, :], lower_i[:, :, :], pair[:, 1, :, :]))
            steps_done()
            step(nc.vector.tensor_reduce(standing, pair[:, 0, :, :], AX.X, ALU.add))
            steps_done()
            ts(chosen, standing, 2.0, None, ALU.is_lt).then_inc(chosen_ready, 1)
            step(ts(first, standing, 0.0, None, ALU.is_equal))
            step(ts(second, standing, 1.0, None, ALU.is_equal))
            dve.wait_ge(rank_done, 1)
            dve.wait_ge(chosen_ready, 1)
            step(stt(rank1, bank[2][0:N, 0:E], 1.0, chosen, ALU.add, ALU.mult))
            steps_done()
            step(ts(jp[:, 0:E], rank1, -1.0, None, ALU.add))
            steps_done()

            def select(job):
                return ts(sel, iota_f[:, :], jp[:, bass.ds(job, 1)], None, ALU.is_equal)

            def select_gated(job):
                return ts(selg, sel[:, None, 0:SLOTS].to_broadcast([N, 4, SLOTS]), jg[:, bass.ds(job, 1)],
                          None, ALU.mult)

            select(0).then_inc(sel_ready, 1)
            step(ts(extra, bank[2][0:N, E:2 * E], float(SLOTS), None, ALU.is_gt))
            step(ts(spare, bank[2][0:N, E:2 * E], float(2 * SLOTS), None, ALU.is_gt))
            step(nc.vector.tensor_reduce(r1[:, 0:1], lg, AX.X, ALU.max))
            step(tt(second_l, second, lg, ALU.mult))
            steps_done()
            step(nc.vector.tensor_reduce(r1[:, 1:2], second_l, AX.X, ALU.add))
            steps_done()
            tt(r1[:, 2:3], r1[:, 1:2], r1[:, 0:1], ALU.subtract).then_inc(gap_ready, 1)
            dve.wait_ge(gather_done, 1)
            nc.vector.tensor_copy(xg[:, 5:8, :], gathered(7, 3)).then_inc(xg_ready, 1)
            dve.wait_ge(gap_exp, 1)
            step(ts(r1[:, 4:5], r1[:, 3:4], 1.0, None, ALU.add))
            steps_done()
            step(nc.vector.reciprocal(r1[:, 5:6], r1[:, 4:5]))
            steps_done()
            step(tt(r1[:, 6:7], r1[:, 5:6], r1[:, 3:4], ALU.mult))
            step(ts(tmp, first, r1[:, 5:6], None, ALU.mult))
            steps_done()
            step(stt(gates, second, r1[:, 6:7], tmp, ALU.mult, ALU.add))
            step(nc.vector.memset(jg[:, E + OVER:], 0.0))
            steps_done()
            step(nc.vector.tensor_copy(jg[:, 0:E], gates))
            steps_done()
            select_gated(0).then_inc(selg_ready, 1)

            step(tt(extra, extra, spare, ALU.add))
            steps_done()
            for e in range(1, E):
                step(tt(start[:, e:e + 1], start[:, e - 1:e], extra[:, e - 1:e], ALU.add))
                steps_done()
            step(tt(spare, start, extra, ALU.add))
            wide = [N, OVER, E]
            own, ge, val, vg = (ov[:, i, :, :] for i in range(4))
            step(tt(ge, kk[:, :, :], start[:, None, :].to_broadcast(wide), ALU.is_ge))
            step(tt(val, start[:, None, :].to_broadcast(wide), kk[:, :, :], ALU.subtract))
            steps_done()
            step(tt(own, kk[:, :, :], spare[:, None, :].to_broadcast(wide), ALU.is_lt))
            steps_done()
            step(tt(own, own, ge, ALU.mult))
            step(ts(val, val, float(SLOTS), -float(SLOTS), ALU.mult, ALU.add))
            steps_done()
            step(tt(val, val, rank1[:, None, :].to_broadcast(wide), ALU.add))
            step(tt(vg, own, gates[:, None, :].to_broadcast(wide), ALU.mult))
            steps_done()
            step(tt(val, val, own, ALU.mult))
            steps_done()
            step(nc.vector.tensor_reduce(ot[:, 0, :], val, AX.X, ALU.add))
            step(nc.vector.tensor_reduce(jg[:, E:E + OVER], vg, AX.X, ALU.add))
            step(nc.vector.memset(jp[:, E + OVER:], -1.0))
            step(nc.vector.tensor_copy(ge, iota_f[:, None, 0:E].to_broadcast(wide)))
            step(nc.vector.tensor_reduce(r1[:, 9:10], extra, AX.X, ALU.add))
            steps_done()
            step(ts(jp[:, E:E + OVER], ot[:, 0, :], -1.0, None, ALU.add))
            step(tt(ge, ge, own, ALU.mult))
            step(ts(r1[:, 10:11], r1[:, 9:10], float(E), None, ALU.add))
            steps_done()
            step(nc.vector.tensor_reduce(ot[:, 1, :], ge, AX.X, ALU.add))
            step(nc.vector.tensor_copy(table[0:1, 0:1], r1[0:1, 10:11]))
            steps_done()
            nc.vector.tensor_copy(table[0:1, 1:1 + OVER], ot[0:1, 1, :]).then_inc(table_ready, 1)
            dve.wait_ge(sct_done, 1)
            nc.vector.tensor_copy(sc[:, :], ps_sc).then_inc(sc_ready, 1)

            dve.wait_ge(table_ready, 1)
            jobs = dve.value_load(table[0:1, 0:1], min_val=E, max_val=E + OVER)
            with dve.Fori(0, jobs) as job:
                for u in range(UNITS):
                    n = job * UNITS + u
                    dve.wait_ge(hT_done, n + 1)
                    nc.vector.tensor_copy(h_T, ps_t[:, :]).then_inc(hT_ready, 1)
                    if u == 0:
                        dve.wait_ge(sct_done, job + 1)
                        select(job + 1).then_inc(sel_ready, 1)
                        dve.wait_ge(sel_ready, job + 2)
                        select_gated(job + 1).then_inc(selg_ready, 1)
                    else:
                        dve.wait_ge(gather_done, job + 2)
                        nc.vector.tensor_copy(xg[:, 5:8, :], gathered(7, 3)).then_inc(xg_ready, 1)
                    dve.wait_ge(chunk_used, n * RING + RING)
                    nc.vector.tensor_copy(y_s[:, HALF:D], ps_y[1][:, :]).then_inc(y_ready[1], 1)
                for d in range(2):
                    dve.wait_ge(scat_done[d], job * UNITS + UNITS)
                dve.wait_ge(sct_done, job + 2)
                nc.vector.tensor_copy(sc[:, :], ps_sc).then_inc(sc_ready, 1)
            dve.wait_ge(scat_done[1], jobs * UNITS)
            nc.vector.tensor_copy(out_s[:, HALF:D], ps_o[1][0:N, :]).then_inc(out_ready[1], 1)

        @block.tensor
        def _(pe):
            mm = nc.tensor.matmul

            def chunk_tile(g, k):
                return slot(gslot(g)).rearrange("p (k n) -> p k n", k=KT)[:, k, :]

            def project_T(m, actT, out_banks, chunks=range(GC)):
                for h in chunks:
                    g = GC * m + h
                    pe.wait_ge(gnn_in[g], 16)
                    for t in range(2):
                        c = P * (2 * (h % 2) + t)
                        for k in range(KT):
                            last = mm(bank[out_banks[h // 2]][:, c:c + N], chunk_tile(g, k)[:, P * t:P * t + P],
                                      actT[:, k, :], start=(k == 0), stop=(k == KT - 1))
                    last.then_inc(gnn_used, 1)

            def project(m, actT, done):
                for h in range(GC):
                    g = GC * m + h
                    pe.wait_ge(gnn_in[g], 16)
                    c = CW * (h % 2)
                    for k in range(KT):
                        last = mm(bank[2 + h // 2][0:N, c:c + CW], actT[:, k, :], chunk_tile(g, k), start=(k == 0),
                                  stop=(k == KT - 1))
                    last.then_inc(done, 1)
                    pe.wait_ge(done, h + 1)
                    pe.nop().then_inc(gnn_used, 1)

            def transposes(src, dst_banks, rows_in, done, src_ready):
                for b in range(2):
                    pe.wait_ge(src_ready, b + 1)
                    for t in range(4):
                        last = nc.tensor.transpose(bank[dst_banks[b]][:, P * t:P * t + rows_in],
                                                   src[:, P * (4 * b + t):P * (4 * b + t + 1)], ident[0:N, 0:N])
                    last.then_inc(done, 1)

            def map_groups(groups):
                for g in groups:
                    b = bank[g % 4]
                    if g >= 4:
                        pe.wait_ge(map_read, g - 3)
                    for t in range(g * EG, min(EC, g * EG + EG)):
                        c = (t - g * EG) * N
                        last = mm(b[0:N, c:c + N], src1h[:, t, :], dst1h[:, t, :], start=True, stop=True)
                    last.then_inc(map_done, 1)

            pe.wait_ge(const_ready, 6)
            transposes(xn, (0, 1), N, xT_done, xn_ready)
            pe.wait_ge(xT_ready, 2)
            project_T(Q, xT, (2, 3), (0,))
            pe.wait_ge(rows_ready, 1)
            for g in range(NG):
                if g % 2 == 0 and g:
                    project_T(Q, xT, (2, 3), (g // 2,))
                a, n = g * EG, min(EG, EC - g * EG)
                if g >= 2:
                    pe.wait_ge(same_done, g - 1)
                mm(bank[g % 2][0:N, 0:n * N], pair16[:, :], rows16[:, a * N:(a + n) * N], start=True,
                   stop=True).then_inc(cell_done, 1)
            project_T(K, xT, (4, 5))
            pe.wait_ge(same_done, NG)
            pe.wait_ge(code_ready, 1)
            pe.wait_ge(proj_read, 2)
            map_groups(range(4))
            project_T(Q2, qvT, (6, 7), (0,))
            map_groups(range(4, NG))
            project_T(Q2, qvT, (6, 7), (1, 2, 3))
            pe.wait_ge(proj_read, 4)
            pe.wait_ge(map_read, NG)
            project_T(K2, koT, (2, 3))
            project_T(V, xT, (4, 5))
            pe.wait_ge(proj_read, 8)
            for b in range(4):
                for c in range(4):
                    h = 8 * (b // 2) + 2 * c + b % 2
                    r = slice(HD * (h % 2), HD * (h % 2) + HD)
                    last = mm(bank[(0, 1, 6, 7)[b]][0:N, P * c:P * c + N], q2Tv[r, h // 2, :], k2Tv[r, h // 2, :],
                              start=True, stop=True)
                last.then_inc(score_done, 1)
            pe.wait_ge(proj_read, 10)
            project(V2, qvT, v2_done)
            for b in range(4):
                pe.wait_ge(probs_ready, b + 1)
                for c in range(4):
                    last = nc.tensor.transpose(bank[(0, 1, 6, 7)[b]][0:N, P * c:P * c + N], attnv[:, 4 * b + c, :],
                                               ident[0:N, 0:N])
                last.then_inc(probsT_done, 1)
            pe.wait_ge(v2_ready, 2)
            for half in range(2):
                for par in range(2):
                    b = 2 * half + par
                    pe.wait_ge(probsT_ready, b + 1)
                    for c in range(4):
                        h = 8 * half + 2 * c + par
                        last = mm(bank[4 + half][HD * par:HD * par + HD, P * c:P * c + N],
                                  v2[:, HD * h:HD * h + HD], attnTv[:, 4 * b + c, :], start=True, stop=True)
                last.then_inc(pv_done, 1)
            pe.wait_ge(oT_ready, 2)
            project(O, koT, o_done)
            pe.wait_ge(x2_ready, 2)
            for h in range(2):
                mm(ps_o[h][0:N, :], ident[0:N, 0:N], x2[:, h * HALF:(h + 1) * HALF], start=True, stop=False,
                   skip_group_check=True)
            transposes(xn, (0, 1), N, x3T_done, x3_ready)
            pe.wait_ge(x3T_ready, 2)
            pe.wait_ge(gate_in, 16)
            for k in range(KT):
                last = mm(bank[6][0:N, 0:E], xT[:, k, :], gate_w[:, k, :], start=(k == 0), stop=(k == KT - 1))
            last.then_inc(logit_done, 1)
            pe.wait_ge(chosen_ready, 1)
            mm(bank[2][0:N, 0:E], upper[:, :], rt[:, 6, :], start=True, stop=True)
            mm(bank[2][0:N, E:2 * E], ones[:, :], rt[:, 6, :], start=True, stop=True).then_inc(rank_done, 1)

            def gather():
                for k in range(KT):
                    b, c = gather_at[k]
                    last = mm(bank[b][:, c:c + N], xn[:, k * P:(k + 1) * P], sel, start=True, stop=True)
                last.then_inc(gather_done, 1)

            def scatter_matrix():
                mm(ps_sc, selg.rearrange("p c s -> p (c s)"), ident[0:N, 0:N], start=True,
                   stop=True).then_inc(sct_done, 1)

            def unit(job, u, slots, landed, between=()):
                n = job * UNITS + u
                if u == 0:
                    pe.wait_ge(xg_ready, job * 2 + 2)
                for k in range(W1C):
                    pe.wait_ge(ring_in[slots[k]], landed[k])
                    w = slot(slots[k])
                    for j in range(4):
                        last = mm(ps_h[SLOTS * j:SLOTS * (j + 1), :], xg[:, k, :], w[:, HALF * j:HALF * (j + 1)],
                                  start=(k == 0), stop=(k == W1C - 1))
                    last.then_inc(chunk_used, 1)
                if u == 0 and isinstance(job, int):
                    pe.wait_ge(selg_ready, 1)
                    scatter_matrix()
                pe.wait_ge(h_ready, n + 1)
                for c in range(CT):
                    last = nc.tensor.transpose(ps_t[:, P * c:P * c + P], h_s[:, P * c:P * c + P], ident[:, :])
                last.then_inc(hT_done, 1)
                if u == UNITS - 1:
                    pe.wait_ge(selg_ready, job + 2)
                    pe.wait_ge(sc_ready, job + 1)
                    scatter_matrix()
                    pe.wait_ge(sel_ready, job + 2)
                    gather()
                pe.wait_ge(hT_ready, n + 1)

                def scatter(d):
                    pe.wait_ge(y_ready[d], n + 1)
                    mm(ps_o[d][0:N, :], sc[:, :], y_s[:, HALF * d:HALF * (d + 1)], start=False, stop=False,
                       skip_group_check=True).then_inc(scat_done[d], 1)

                for i in range(W2C):
                    d, c = i // CT, i % CT
                    pe.wait_ge(ring_in[slots[W1C + i]], landed[W1C + i])
                    w = slot(slots[W1C + i]).rearrange("p (j d) -> p j d", d=HALF)
                    for j in range(4):
                        last = mm(ps_y[d][SLOTS * j:SLOTS * (j + 1), :], h_T[:, P * c + SLOTS * j:P * c + SLOTS * (j + 1)],
                                  w[:, j, :], start=(c == 0), stop=(c == CT - 1))
                    last.then_inc(chunk_used, 1)
                    if i == CT + 1:
                        if u == 0:
                            pe.wait_ge(sc_ready, job + 1)
                        scatter(0)
                scatter(1)

            pe.wait_ge(sel_ready, 1)
            gather()
            for u in range(UNITS):
                order = range(RING * u, RING * (u + 1))
                unit(0, u, [first_slot(c) for c in order], [16 * (c // SLOTS_ALL + 1) for c in order])
            pe.wait_ge(table_ready, 1)
            jobs = pe.value_load(table[0:1, 0:1], min_val=E, max_val=E + OVER)
            with pe.Fori(1, jobs) as job:
                for u in range(UNITS):
                    n = job * UNITS + u
                    unit(job, u, range(RING), [n * 16 + (16 if c < AGAIN else 0) for c in range(RING)])


def _col_layout(w):
    return w.T.reshape(KT, P, GC, CW).transpose(2, 1, 0, 3).reshape(GC, P, CHUNK)


def _layout(a):
    w = {k: np.asarray(v) for k, v in a.items()}
    g = {k[7:]: v for k, v in w.items() if k.startswith("L0_gnn_")}
    gnn = np.concatenate([_col_layout(g[k]) for k in ("wq", "wk", "wiq", "wik", "wv", "wiv", "wo")])
    colb = np.stack([g[k] for k in ("bq", "bk", "biq", "bik", "bv")]).reshape(5, KT, P).transpose(2, 0, 1)
    edges = np.stack([w["src"], w["dst"], w["edge_type_5"]])
    w1 = w["L0_ffn_w1"].reshape(E, UNITS, UF, KT, P).transpose(0, 1, 3, 4, 2)
    w2 = w["L0_ffn_w2"].reshape(E, 2, HALF, UNITS, 4, CT, P).transpose(0, 3, 1, 5, 6, 4, 2)
    return {
        "x": w["x"],
        "rows": edges[0:2],
        "cols": edges.reshape(3, EC, N).transpose(2, 0, 1),
        "etw": g["edge_type_weights"].reshape(1, 4),
        "gnn_w": gnn,
        "colb": colb,
        "biv": g["biv"].reshape(1, D),
        "bo": g["bo"].reshape(1, D),
        "gate": w["L0_ffn_gate_w"].T.reshape(KT, P, E).transpose(1, 0, 2),
        "w1": w1.reshape(E, UNITS, W1C, P, CHUNK),
        "w2": w2.reshape(E, UNITS, W2C, P, CHUNK),
    }


def kernel(**inputs):
    import concourse.bacc as bacc
    from concourse.bass_utils import run_bass_kernel_spmd

    nc = bacc.Bacc("TRN2", target_bir_lowering=False, num_devices=1)
    arrays, args = {}, []
    for name, a in _layout(inputs).items():
        a = np.ascontiguousarray(a)
        arrays[f"in_{name}"] = a
        args.append(nc.dram_tensor(f"in_{name}", a.shape, mybir.dt.from_np(a.dtype), kind="ExternalInput").ap())
    out = nc.dram_tensor("out_0", (N, D), F32, kind="ExternalOutput").ap()
    gnn_moe_kernel(nc, *args, out)
    r = run_bass_kernel_spmd(nc, [arrays], core_ids=[0])
    return r.results[0]["out_0"]
```

```python
from contextlib import ExitStack

import numpy as np

import concourse.bass as bass
from concourse import mybir

F32 = mybir.dt.float32
F16 = mybir.dt.float16
I32 = mybir.dt.int32
ALU = mybir.AluOpType
ACT = mybir.ActivationFunctionType
AX = mybir.AxisListType

P = 128
N = 96
D = 1024
KT = D // P
HEADS = 16
HD = D // HEADS
E = 8
F = 4 * D
EDGES = 3168
EC = EDGES // N
EG = 5
NG = -(-EC // EG)
HALF = 512
SLOTS = 32
OVER = (2 * N) // (SLOTS + 1)
JOBS = E + OVER + 1
UNITS = 2
UF = F // UNITS
CT = UF // P // 4
CHUNK = 2048
W1C = KT * UF // CHUNK
W2C = (UF // P) * D // CHUNK
RING = 16
EXTRA = 4
LATE = 2
GSLOTS = RING + EXTRA
SLOTS_ALL = GSLOTS + LATE
PER_JOB = UNITS * (W1C + W2C)
AGAIN = PER_JOB - SLOTS_ALL
EPS = 1e-5
FAR = -1e30
SCALE = 1.0 / 8.0
SHIFT = 8
assert EC * N == EDGES and W1C + W2C == RING and HD * HEADS == D and SCALE * SCALE * HD == 1.0
assert UF == 4 * HALF and CT * 4 * P == UF and W1C == KT and W2C == 2 * CT and 0 < AGAIN <= RING

Q, K, Q2, K2, V, V2, O = range(7)
GC = 4
CW = D // GC
NGC = 7 * GC
assert NG // 2 + 1 == GC


def gslot(g):
    return (g - (NGC - GSLOTS)) % GSLOTS


def first_slot(c):
    return c % SLOTS_ALL


def gnn_moe_kernel(nc, x_d, rows_d, cols_d, etw_d, gnn_w_d, colb_d, biv_d, bo_d, gate_d, w1_d, w2_d, out_d):
    with ExitStack() as ctx:
        def sb(name, shape, dt=F32):
            return ctx.enter_context(nc.sbuf_tensor(name, shape, dt))

        def sem(name):
            return ctx.enter_context(nc.semaphore(name))

        ring = sb("ring", [P, GSLOTS * CHUNK])
        heads = sb("heads", [P, 3 * HEADS * N])
        assert 3 * HEADS * N >= LATE * CHUNK and 2 * KT * N == HEADS * N

        def slot(s, n=1):
            if s >= GSLOTS:
                return heads[:, (s - GSLOTS) * CHUNK:(s - GSLOTS + n) * CHUNK]
            return ring[:, s * CHUNK:(s + n) * CHUNK]

        rows_i = slot(6, 2)[0:2, 0:EDGES].bitcast(I32)
        early = slot(8, 4).bitcast(F16)
        rows16 = early[0:2, 0:EDGES]
        same = early[0:N, EDGES:2 * EDGES].rearrange("p (t j) -> p t j", j=N)
        src1h = early[0:N, 2 * EDGES:3 * EDGES].rearrange("p (t j) -> p t j", j=N)
        dst1h = early[0:N, 3 * EDGES:4 * EDGES].rearrange("p (t j) -> p t j", j=N)
        x_s = sb("x_s", [P, D])
        x = x_s[0:N, :]
        xn = sb("xn", [N, D])
        x2 = sb("x2", [N, D])
        xT_s = sb("xT", [P, KT * N])
        qvT_s = sb("qvT", [P, KT * N])
        koT_s = sb("koT", [P, KT * N])
        qk2T, attn, attnT = (heads[:, i * HEADS * N:(i + 1) * HEADS * N] for i in range(3))
        xT, qvT, koT, q2T, k2T = (t.rearrange("p (k n) -> p k n", n=N) for t in (
            xT_s[:, :], qvT_s[:, :], koT_s[:, :], qk2T[:, 0:KT * N], qk2T[:, KT * N:]))
        v2 = qk2T[0:N, 0:D]
        probs = attn[0:N, :].rearrange("p (h m) -> p h m", m=N)
        probsT = attnT[0:N, :].rearrange("p (h m) -> p h m", m=N)
        bo_row, biv_row = attn[0:1, 0:D], attnT[0:1, 384:384 + D]
        h_s, h_T = qvT_s[:, 0:HALF], koT_s[:, 0:HALF]
        y_s, out_s = x_s, x2
        assert KT * N >= KT * SLOTS + 2 * E * E + N + P + 4 * OVER * E
        cuts = np.cumsum([0, KT * SLOTS, 2 * E * E, N, P, 4 * OVER * E])
        xg, pair, sel, selg, ov = (xT_s[:, a:b] for a, b in zip(cuts[:-1].tolist(), cuts[1:].tolist()))
        xg = xg.rearrange("p (k s) -> p k s", s=SLOTS)
        pair = pair[0:N, :].rearrange("p (i e f) -> p i e f", i=2, f=E)
        sel = sel[0:N, :]
        selg = selg[0:N, :].rearrange("p (c s) -> p c s", s=SLOTS)
        ov = ov[0:N, :].rearrange("p (i k e) -> p i k e", i=4, e=E)

        ident = sb("ident", [P, P])
        upper = sb("upper", [N, N])
        ones = sb("ones", [N, N])
        tri16 = sb("tri16", [N, N], F16)
        iota_i = sb("iota_i", [N, N], I32)
        iota_f = sb("iota_f", [N, N])
        iota16 = sb("iota16", [N, N], F16)
        code_i = sb("code_i", [N, EC], I32)
        pair16 = sb("pair16", [2, N], F16)
        cols_i = sb("cols_i", [N, 3, EC], I32)
        cols = sb("cols", [N, 3, EC])
        cols16 = sb("cols16", [N, 3, EC], F16)
        ec = sb("ec", [N, 6, EC])
        kv16 = sb("kv16", [N, EC], F16)
        merged, mtmp = attnT[0:N, 0:N], attnT[0:N, N:2 * N]
        mcode_i = attnT[0:N, 2 * N:3 * N].bitcast(I32)
        mask = sb("mask", [N, N])
        etw = sb("etw", [N, 4])
        sp = sb("sp", [N, 4, 4])
        colb = sb("colb", [P, 5, KT])
        gate_w = sb("gate_w", [P, KT * E + N])
        stat = sb("stat", [N, 2, 6])
        mv = sb("mv", [N, 2])
        std = sb("std", [N, 1])
        rstd = sb("rstd", [N, 1])
        smx = sb("smx", [N, 4, 4])
        ssum = sb("ssum", [N, 4, 4])
        warm = sb("warm", [1, 1])
        rt = sb("rt", [N, 11, E])
        chosen_s = sb("chosen", [N, E])
        chosen = chosen_s[:, :]
        r1 = sb("r1", [N, 11])
        kk = sb("kk", [N, OVER, E])
        sc = sb("sc", [P, N])
        lower_i = sb("lower_i", [N, E, E], I32)
        jp = sb("jp", [N, JOBS])
        jg = sb("jg", [N, JOBS])
        ot = sb("ot", [N, 3, OVER])
        table = sb("table", [1, 1 + OVER], I32)

        bank = [ctx.enter_context(nc.psum_tensor(f"bank{b}", [P, HALF], F32)) for b in range(8)]
        ps_h, ps_t, ps_y, ps_o = bank[0], bank[1], bank[2:4], bank[4:6]

        def quarter(b, rows=P, n=4):
            return b[0:rows, :].rearrange("p (q c) -> p q c", c=P)[:, 0:n, 0:N]

        def edge_bank(b, t):
            return b[0:N, 0:t * N].rearrange("p (t j) -> p t j", j=N)

        gather_at = [(6, N * k) if k < 5 else (7, N * (k - 5)) for k in range(KT)]

        def gathered(b, n):
            return bank[b][:, 0:n * N].rearrange("p (k c) -> p k c", c=N)[:, :, 0:SLOTS]

        ps_sc = bank[7][:, 384:384 + N]
        assert 3 * N <= 384 and 5 * N <= HALF

        x_in, rows_in, cols_in, etw_in, colb_in, gate_in, biv_in, bo_in = (
            sem(s) for s in ("x_in", "rows_in", "cols_in", "etw_in", "colb_in", "gate_in", "biv_in", "bo_in"))
        gnn_in = [sem(f"gnn_in{g}") for g in range(NGC)]
        ring_in = [sem(f"ring_in{s}") for s in range(SLOTS_ALL)]
        gnn_used = sem("gnn_used")
        chunk_used = sem("chunk_used")
        const_ready = sem("const_ready")
        pool_step = sem("pool_step")
        dve_step = sem("dve_step")
        act_step = sem("act_step")
        var_ready, std_ready = sem("var_ready"), sem("std_ready")
        xn_ready, xT_done, xT_ready = sem("xn_ready"), sem("xT_done"), sem("xT_ready")
        x3_ready, x3T_done, x3T_ready = sem("x3_ready"), sem("x3T_done"), sem("x3T_ready")
        bo_ready, biv_ready = sem("bo_ready"), sem("biv_ready")
        rows_ready = sem("rows_ready")
        cell_done, same_done = sem("cell_done"), sem("same_done")
        code_ready = sem("code_ready")
        map_done, map_read = sem("map_done"), sem("map_read")
        etw_abs, etw_exp, etw_ln = sem("etw_abs"), sem("etw_exp"), sem("etw_ln")
        proj_read = sem("proj_read")
        score_done, score_sub, score_exp = sem("score_done"), sem("score_sub"), sem("score_exp")
        probs_ready, probsT_done, probsT_ready = sem("probs_ready"), sem("probsT_done"), sem("probsT_ready")
        v2_ready = sem("v2_ready")
        pv_done, oT_ready = sem("pv_done"), sem("oT_ready")
        x2_ready = sem("x2_ready")
        logit_done, gap_ready, gap_exp = sem("logit_done"), sem("gap_ready"), sem("gap_exp")
        warm_ready = sem("warm_ready")
        chosen_ready, rank_done, count_done = sem("chosen_ready"), sem("rank_done"), sem("count_done")
        table_ready = sem("table_ready")
        sel_ready, selg_ready = sem("sel_ready"), sem("selg_ready")
        gather_done, xg_ready = sem("gather_done"), sem("xg_ready")
        sct_done, sc_ready = sem("sct_done"), sem("sc_ready")
        h_ready, hT_done, hT_ready = sem("h_ready"), sem("hT_done"), sem("hT_ready")
        y_ready = [sem("y_ready0"), sem("y_ready1")]
        scat_done = [sem("scat_done0"), sem("scat_done1")]
        out_ready = [sem("out_ready0"), sem("out_ready1")]
        stored = sem("stored")

        block = ctx.enter_context(nc.Block())

        @block.sync
        def _(sp_):
            sp_.dma_start(x, x_d).then_inc(x_in, 16)
            for g in range(NGC):
                if gslot(g) == 6:
                    sp_.wait_ge(rows_ready, 1)
                if gslot(g) == 8:
                    sp_.wait_ge(map_done, NG)
                if g >= GSLOTS:
                    sp_.wait_ge(gnn_used, g - GSLOTS + 1)
                sp_.dma_start(slot(gslot(g)), gnn_w_d[g]).then_inc(gnn_in[g], 16)

            def expert_chunk(expert, c, s):
                u, r = c // RING, c % RING
                src = w1_d[expert, u, r] if r < W1C else w2_d[expert, u, r - W1C]
                sp_.dma_start(slot(s), src).then_inc(ring_in[s], 16)

            for c in range(PER_JOB):
                if c < GSLOTS:
                    sp_.wait_ge(gnn_used, NGC - GSLOTS + c + 1)
                elif c < SLOTS_ALL:
                    sp_.wait_ge(pv_done, 2)
                else:
                    sp_.wait_ge(chunk_used, c - SLOTS_ALL + 1)
                expert_chunk(0, c, first_slot(c))
            for c in range(PER_JOB):
                before = SLOTS_ALL + c if c < AGAIN else c if c < RING else PER_JOB + c - RING
                sp_.wait_ge(chunk_used, before + 1)
                expert_chunk(1, c, c % RING)
            with sp_.Fori(2, E) as e:
                for c in range(PER_JOB):
                    sp_.wait_ge(chunk_used, e * PER_JOB + (c - RING + 1))
                    expert_chunk(e, c, c % RING)
            sp_.wait_ge(table_ready, 1)
            jobs = sp_.value_load(table[0:1, 0:1], min_val=E, max_val=E + OVER)
            with sp_.If(jobs > E):
                with sp_.Fori(E, jobs) as job:
                    e = sp_.value_load(table[0:1, bass.ds(job - (E - 1), 1)], min_val=0, max_val=E - 1)
                    for c in range(PER_JOB):
                        sp_.wait_ge(chunk_used, job * PER_JOB + (c - RING + 1))
                        expert_chunk(e, c, c % RING)
            for d in range(2):
                sp_.wait_ge(out_ready[d], 1)
                sp_.dma_start(out_d[:, HALF * d:HALF * (d + 1)], out_s[:, HALF * d:HALF * (d + 1)]).then_inc(stored, 16)
            sp_.wait_ge(stored, 32)

        @block.gpsimd
        def _(pool):
            pool.dma_start(cols_i[:, :, :], cols_d).then_inc(cols_in, 16)
            pool.memset(ones[:, :], 1.0).then_inc(pool_step, 1)
            pool.memset(ident[:, :], 1.0).then_inc(pool_step, 1)
            pool.memset(pair16[:, :], 1.0).then_inc(pool_step, 1)
            pool.iota(iota_i[:, :], [[1, N]], base=0, channel_multiplier=0).then_inc(pool_step, 1)
            pool.iota(code_i[:, :], [[SHIFT, EC]], base=0, channel_multiplier=0).then_inc(pool_step, 1)
            pool.wait_ge(pool_step, 5)
            pool.affine_select(out=ident[:, :], in_=ident[:, :], compare_op=ALU.is_equal, fill=0.0, base=0,
                               pattern=[[1, P]], channel_multiplier=-1).then_inc(const_ready, 1)
            pool.affine_select(out=upper[:, :], in_=ones[:, :], compare_op=ALU.is_gt, fill=0.0, base=0,
                               pattern=[[1, N]], channel_multiplier=-1).then_inc(const_ready, 1)
            pool.memset(pair16[0:1, :], float(N)).then_inc(const_ready, 1)
            pool.tensor_copy(iota_f[:, :], iota_i[:, :]).then_inc(const_ready, 1)
            pool.tensor_copy(iota16[:, :], iota_i[:, :]).then_inc(const_ready, 1)
            pool.wait_ge(const_ready, 5)
            pool.tensor_copy(tri16[:, :], upper[:, :]).then_inc(const_ready, 1)
            pool.iota(lower_i[:, :, :], [[1, E], [-1, E]], base=0, channel_multiplier=0).then_inc(const_ready, 1)
            pool.memset(gate_w[:, KT * E:], 0.0).then_inc(const_ready, 1)
            pool.wait_ge(bo_in, 16)
            pool.partition_broadcast(x2[:, :], bo_row, N).then_inc(bo_ready, 1)
            pool.wait_ge(biv_in, 16)
            pool.wait_ge(xT_done, 2)
            pool.partition_broadcast(xn[:, :], biv_row, N).then_inc(biv_ready, 1)

        @block.scalar
        def _(act):
            act.dma_start(rows_i, rows_d).then_inc(rows_in, 16)
            act.dma_start(etw[:, :], etw_d.to_broadcast([N, 4])).then_inc(etw_in, 16)
            act.dma_start(colb[:, :, :], colb_d).then_inc(colb_in, 16)
            act.dma_start(gate_w[:, 0:KT * E], gate_d).then_inc(gate_in, 16)
            act.dma_start(bo_row, bo_d).then_inc(bo_in, 16)
            act.dma_start(biv_row, biv_d).then_inc(biv_in, 16)

            def root(n):
                act.wait_ge(var_ready, n)
                nc.scalar.activation(std[:, :], mv[:, 1:2], ACT.Sqrt, bias=EPS).then_inc(std_ready, 1)

            act.wait_ge(warm_ready, 1)
            nc.scalar.activation(warm[:, :], warm[:, :], ACT.Sqrt).then_inc(act_step, 1)
            root(1)
            for b in range(2):
                act.wait_ge(xT_done, b + 1)
                nc.scalar.copy(xT[:, 4 * b:4 * b + 4, :], quarter(bank[b])).then_inc(xT_ready, 1)
            act.wait_ge(etw_abs, 1)
            nc.scalar.activation(sp[:, 1, :], sp[:, 0, :], ACT.Exp).then_inc(etw_exp, 1)
            act.wait_ge(etw_exp, 1)
            nc.scalar.activation(sp[:, 2, :], sp[:, 1, :], ACT.Ln, bias=1.0).then_inc(etw_ln, 1)
            act.wait_ge(colb_in, 16)
            banks = {Q: (2, 3), K: (4, 5), Q2: (6, 7), K2: (2, 3), V: (4, 5)}
            outs = {Q: qvT, K: koT, Q2: q2T, V: qvT, K2: k2T}
            for m in (Q, K, Q2, K2, V):
                for h in range(2):
                    act.wait_ge(gnn_used, GC * m + 2 * h + 2)
                    for t in range(4 * h, 4 * h + 4):
                        c = P * (t % 4)
                        last = nc.scalar.activation(outs[m][:, t, :], bank[banks[m][t // 4]][:, c:c + N],
                                                    ACT.Identity, bias=colb[:, m, t:t + 1])
                    last.then_inc(proj_read, 1)
            for b in range(4):
                act.wait_ge(score_sub, b + 1)
                s = probs[:, 4 * b:4 * b + 4, :]
                nc.scalar.activation(s, s, ACT.Exp).then_inc(score_exp, 1)
            act.wait_ge(biv_ready, 1)
            for b in range(4):
                act.wait_ge(probsT_done, b + 1)
                nc.scalar.copy(probsT[:, 4 * b:4 * b + 4, :], quarter(bank[(0, 1, 6, 7)[b]], N)).then_inc(probsT_ready, 1)
            for b in range(2):
                act.wait_ge(pv_done, b + 1)
                nc.scalar.copy(koT[:, 4 * b:4 * b + 4, :], quarter(bank[4 + b])).then_inc(oT_ready, 1)
            nc.scalar.activation(warm[:, :], warm[:, :], ACT.Sqrt).then_inc(act_step, 1)
            root(2)
            act.wait_ge(x3T_done, 1)
            nc.scalar.copy(xT[:, 0:4, :], quarter(bank[0])).then_inc(x3T_ready, 1)
            act.wait_ge(gap_ready, 1)
            nc.scalar.activation(r1[:, 3:4], r1[:, 2:3], ACT.Exp).then_inc(gap_exp, 1)
            act.wait_ge(gather_done, 1)
            nc.scalar.copy(xg[:, 0:5, :], gathered(6, 5)).then_inc(xg_ready, 1)
            act.wait_ge(table_ready, 1)
            jobs = act.value_load(table[0:1, 0:1], min_val=E, max_val=E + OVER)
            with act.Fori(0, jobs) as job:
                for u in range(UNITS):
                    n = job * UNITS + u
                    act.wait_ge(chunk_used, n * RING + W1C)
                    nc.scalar.activation(h_s, ps_h[:, :], ACT.Relu).then_inc(h_ready, 1)
                    if u == UNITS - 1:
                        act.wait_ge(gather_done, job + 2)
                        nc.scalar.copy(xg[:, 0:5, :], gathered(6, 5)).then_inc(xg_ready, 1)
                    act.wait_ge(chunk_used, n * RING + W1C + CT)
                    nc.scalar.copy(y_s[:, 0:HALF], ps_y[0][:, :]).then_inc(y_ready[0], 1)
            act.wait_ge(scat_done[0], jobs * UNITS)
            nc.scalar.copy(out_s[:, 0:HALF], ps_o[0][0:N, :]).then_inc(out_ready[0], 1)

        @block.vector
        def _(dve):
            count = [0]

            def step(ins):
                count[0] += 1
                return ins.then_inc(dve_step, 1)

            def steps_done():
                dve.wait_ge(dve_step, count[0])

            tt, ts, stt = nc.vector.tensor_tensor, nc.vector.tensor_scalar, nc.vector.scalar_tensor_tensor

            def half_stats(src, h):
                step(nc.vector.bn_stats(stat[:, h, :], src[:, h * HALF:(h + 1) * HALF]))

            def layernorm(n, src, done):
                steps_done()
                nc.vector.bn_aggr(mv[:, :], stat[:, :, :].rearrange("p a b -> p (a b)")).then_inc(var_ready, 1)
                dve.wait_ge(std_ready, n)
                step(nc.vector.reciprocal(rstd[:, :], std[:, :]))
                steps_done()
                for h in range(2):
                    half = slice(h * HALF, (h + 1) * HALF)
                    ts(xn[:, half], src[:, half], mv[:, 0:1], rstd[:, 0:1], ALU.subtract, ALU.mult).then_inc(done, 1)

            nc.vector.memset(warm[:, :], 1.0).then_inc(warm_ready, 1)
            dve.wait_ge(x_in, 16)
            half_stats(x, 0)
            half_stats(x, 1)
            layernorm(1, x, xn_ready)

            dve.wait_ge(etw_in, 16)
            step(ts(sp[:, 3, :], etw[:, :], -1.0, None, ALU.mult))
            steps_done()
            step(tt(sp[:, 3, :], sp[:, 3, :], etw[:, :], ALU.max))
            steps_done()
            ts(sp[:, 0, :], sp[:, 3, :], -1.0, None, ALU.mult).then_inc(etw_abs, 1)
            dve.wait_ge(etw_abs, 1)
            step(ts(sp[:, 3, :], etw[:, :], 0.0, None, ALU.max))

            dve.wait_ge(rows_in, 16)
            nc.vector.tensor_copy(rows16, rows_i).then_inc(rows_ready, 1)
            dve.wait_ge(cols_in, 16)
            step(nc.vector.tensor_copy(cols[:, :, :], cols_i[:, :, :]))
            step(nc.vector.tensor_copy(cols16[:, :, :], cols_i[:, :, :]))
            dve.wait_ge(const_ready, 8)
            dve.wait_ge(rows_ready, 1)
            steps_done()
            cell, cls, code, dup, keep, t8 = (ec[:, i, :] for i in range(6))
            step(stt(cell, cols[:, 0, :], float(N), cols[:, 1, :], ALU.mult, ALU.add))
            step(ts(cls, cols[:, 2, :], 0.0, 4.0, ALU.is_equal, ALU.mult))
            step(nc.vector.tensor_copy(t8, code_i[:, :]))
            steps_done()
            step(tt(cls, cls, cols[:, 2, :], ALU.add))
            for one_hot, end in ((dst1h, 1), (src1h, 0)):
                step(tt(one_hot, iota16[:, None, :].to_broadcast([N, EC, N]),
                        cols16[:, end, :, None].to_broadcast([N, EC, N]), ALU.is_equal))
            for g in range(NG):
                a, n = g * EG, min(EG, EC - g * EG)
                dve.wait_ge(cell_done, g + 1)
                ins = tt(same[:, a:a + n, :], edge_bank(bank[g % 2], n),
                         cell[:, a:a + n, None].to_broadcast([N, n, N]), ALU.is_equal)
                ins.then_inc(same_done, 1)
            dve.wait_ge(same_done, NG)
            step(tt(same, same, tri16[:, None, :].to_broadcast([N, EC, N]), ALU.mult))
            steps_done()
            step(nc.vector.tensor_reduce(dup, same, AX.X, ALU.max))
            step(tt(code, cls, t8, ALU.add))
            steps_done()
            step(ts(keep, dup, -1.0, 1.0, ALU.mult, ALU.add))
            steps_done()
            step(tt(kv16[:, :], code, keep, ALU.mult))
            steps_done()
            tt(dst1h, dst1h, kv16[:, :, None].to_broadcast([N, EC, N]), ALU.mult).then_inc(code_ready, 1)
            dve.wait_ge(bo_ready, 1)
            step(tt(x, x, x2[:, :], ALU.add))
            steps_done()
            dve.wait_ge(etw_ln, 1)
            step(tt(etw[:, :], sp[:, 3, :], sp[:, 2, :], ALU.add))
            for g in range(NG):
                n = min(EG, EC - g * EG)
                dve.wait_ge(map_done, g + 1)
                nc.vector.tensor_reduce(mtmp if g else merged, edge_bank(bank[g % 4], n).rearrange("p t j -> p j t"),
                                        AX.X, ALU.max).then_inc(map_read, 1)
                dve.wait_ge(map_read, g + 1)
                if g:
                    step(tt(merged, merged, mtmp, ALU.max))
                    steps_done()
            step(nc.vector.tensor_copy(mcode_i, merged))
            steps_done()
            step(nc.vector.tensor_single_scalar(mcode_i, mcode_i, SHIFT - 1, ALU.bitwise_and))
            steps_done()
            step(nc.vector.tensor_copy(merged, mcode_i))
            steps_done()
            step(stt(mtmp, merged, 0.0, ident[0:N, 0:N], ALU.is_equal, ALU.mult))
            steps_done()
            step(stt(merged, mtmp, 4.0, merged, ALU.mult, ALU.add))
            steps_done()
            step(ts(mask[:, :], merged, 0.0, FAR, ALU.is_equal, ALU.mult))
            for c in range(4):
                step(ts(mtmp, merged, float(c + 1), etw[:, c:c + 1], ALU.is_equal, ALU.mult))
                steps_done()
                step(tt(mask[:, :], mask[:, :], mtmp, ALU.add))
                steps_done()

            for b in range(4):
                s = probs[:, 4 * b:4 * b + 4, :]
                dve.wait_ge(score_done, b + 1)
                step(stt(s, quarter(bank[(0, 1, 6, 7)[b]], N), SCALE, mask[:, None, :].to_broadcast([N, 4, N]),
                         ALU.mult, ALU.add))
                steps_done()
                step(nc.vector.tensor_reduce(smx[:, b, :], s, AX.X, ALU.max))
                steps_done()
                tt(s, s, smx[:, b, :, None].to_broadcast([N, 4, N]), ALU.subtract).then_inc(score_sub, 1)
            for b in range(4):
                s = probs[:, 4 * b:4 * b + 4, :]
                dve.wait_ge(score_exp, b + 1)
                step(nc.vector.tensor_reduce(ssum[:, b, :], s, AX.X, ALU.add))
                steps_done()
                step(nc.vector.reciprocal(ssum[:, b, :], ssum[:, b, :]))
                steps_done()
                tt(s, s, ssum[:, b, :, None].to_broadcast([N, 4, N]), ALU.mult).then_inc(probs_ready, 1)
            dve.wait_ge(biv_ready, 1)
            for h in range(2):
                dve.wait_ge(gnn_used, GC * V2 + 2 * h + 2)
                half = slice(h * HALF, (h + 1) * HALF)
                tt(v2[:, half], bank[2 + h][0:N, :], xn[:, half], ALU.add).then_inc(v2_ready, 1)

            step(nc.vector.tensor_copy(kk[:, :, :], iota_f[:, 0:OVER, None].to_broadcast([N, OVER, E])))
            step(nc.vector.tensor_single_scalar(lower_i[:, :, :], lower_i[:, :, :], 0, ALU.is_gt))
            step(nc.vector.memset(rt[:, 9, 0:1], 0.0))
            for h in range(2):
                dve.wait_ge(gnn_used, GC * O + 2 * h + 2)
                half = slice(h * HALF, (h + 1) * HALF)
                tt(x2[:, half], bank[2 + h][0:N, :], x[:, half], ALU.add).then_inc(x2_ready, 1)
                dve.wait_ge(x2_ready, h + 1)
                half_stats(x2, h)
            dve.wait_ge(v2_ready, 2)
            layernorm(2, x2, x3_ready)
            dve.wait_ge(x3T_done, 2)
            nc.vector.tensor_copy(xT[:, 4:8, :], quarter(bank[1])).then_inc(x3T_ready, 1)

            lg, first, second, standing, tmp, rank1, gates, spare, extra, start, second_l = (
                rt[:, i, :] for i in range(11))
            dve.wait_ge(logit_done, 1)
            step(nc.vector.tensor_copy(lg, bank[6][0:N, 0:E]))
            steps_done()
            square = [N, E, E]
            step(tt(pair[:, 0, :, :], lg[:, None, :].to_broadcast(square), lg[:, :, None].to_broadcast(square),
                    ALU.is_gt))
            step(tt(pair[:, 1, :, :], lg[:, None, :].to_broadcast(square), lg[:, :, None].to_broadcast(square),
                    ALU.is_ge))
            steps_done()
            step(nc.vector.copy_predicated(pair[:, 0, :, :], lower_i[:, :, :], pair[:, 1, :, :]))
            steps_done()
            step(nc.vector.tensor_reduce(standing, pair[:, 0, :, :], AX.X, ALU.add))
            steps_done()
            ts(chosen, standing, 2.0, None, ALU.is_lt).then_inc(chosen_ready, 1)
            step(ts(first, standing, 0.0, None, ALU.is_equal))
            step(ts(second, standing, 1.0, None, ALU.is_equal))
            dve.wait_ge(rank_done, 1)
            dve.wait_ge(chosen_ready, 1)
            step(stt(rank1, bank[2][0:N, 0:E], 1.0, chosen, ALU.add, ALU.mult))
            steps_done()
            step(ts(jp[:, 0:E], rank1, -1.0, None, ALU.add))
            steps_done()

            def select(job):
                return ts(sel, iota_f[:, :], jp[:, bass.ds(job, 1)], None, ALU.is_equal)

            def select_gated(job):
                return ts(selg, sel[:, None, 0:SLOTS].to_broadcast([N, 4, SLOTS]), jg[:, bass.ds(job, 1)],
                          None, ALU.mult)

            select(0).then_inc(sel_ready, 1)
            dve.wait_ge(count_done, 1)
            step(ts(extra, bank[3][0:N, 0:E], float(SLOTS), None, ALU.is_gt))
            step(ts(spare, bank[3][0:N, 0:E], float(2 * SLOTS), None, ALU.is_gt))
            step(nc.vector.tensor_reduce(r1[:, 0:1], lg, AX.X, ALU.max))
            step(tt(second_l, second, lg, ALU.mult))
            steps_done()
            step(nc.vector.tensor_reduce(r1[:, 1:2], second_l, AX.X, ALU.add))
            steps_done()
            tt(r1[:, 2:3], r1[:, 1:2], r1[:, 0:1], ALU.subtract).then_inc(gap_ready, 1)
            dve.wait_ge(gather_done, 1)
            nc.vector.tensor_copy(xg[:, 5:8, :], gathered(7, 3)).then_inc(xg_ready, 1)
            dve.wait_ge(gap_exp, 1)
            step(ts(r1[:, 4:5], r1[:, 3:4], 1.0, None, ALU.add))
            steps_done()
            step(nc.vector.reciprocal(r1[:, 5:6], r1[:, 4:5]))
            steps_done()
            step(tt(r1[:, 6:7], r1[:, 5:6], r1[:, 3:4], ALU.mult))
            step(ts(tmp, first, r1[:, 5:6], None, ALU.mult))
            steps_done()
            step(stt(gates, second, r1[:, 6:7], tmp, ALU.mult, ALU.add))
            step(nc.vector.memset(jg[:, E + OVER:], 0.0))
            steps_done()
            step(nc.vector.tensor_copy(jg[:, 0:E], gates))
            steps_done()
            select_gated(0).then_inc(selg_ready, 1)

            step(tt(extra, extra, spare, ALU.add))
            steps_done()
            for e in range(1, E):
                step(tt(start[:, e:e + 1], start[:, e - 1:e], extra[:, e - 1:e], ALU.add))
                steps_done()
            step(tt(spare, start, extra, ALU.add))
            wide = [N, OVER, E]
            own, ge, val, vg = (ov[:, i, :, :] for i in range(4))
            step(tt(ge, kk[:, :, :], start[:, None, :].to_broadcast(wide), ALU.is_ge))
            step(tt(val, start[:, None, :].to_broadcast(wide), kk[:, :, :], ALU.subtract))
            steps_done()
            step(tt(own, kk[:, :, :], spare[:, None, :].to_broadcast(wide), ALU.is_lt))
            steps_done()
            step(tt(own, own, ge, ALU.mult))
            step(ts(val, val, float(SLOTS), -float(SLOTS), ALU.mult, ALU.add))
            steps_done()
            step(tt(val, val, rank1[:, None, :].to_broadcast(wide), ALU.add))
            step(tt(vg, own, gates[:, None, :].to_broadcast(wide), ALU.mult))
            steps_done()
            step(tt(val, val, own, ALU.mult))
            steps_done()
            step(nc.vector.tensor_reduce(ot[:, 0, :], val, AX.X, ALU.add))
            step(nc.vector.tensor_reduce(jg[:, E:E + OVER], vg, AX.X, ALU.add))
            step(nc.vector.memset(jp[:, E + OVER:], -1.0))
            step(nc.vector.tensor_copy(ge, iota_f[:, None, 0:E].to_broadcast(wide)))
            step(nc.vector.tensor_reduce(r1[:, 9:10], extra, AX.X, ALU.add))
            steps_done()
            step(ts(jp[:, E:E + OVER], ot[:, 0, :], -1.0, None, ALU.add))
            step(tt(ge, ge, own, ALU.mult))
            step(ts(r1[:, 10:11], r1[:, 9:10], float(E), None, ALU.add))
            steps_done()
            step(nc.vector.tensor_reduce(ot[:, 1, :], ge, AX.X, ALU.add))
            step(nc.vector.tensor_copy(table[0:1, 0:1], r1[0:1, 10:11]))
            steps_done()
            nc.vector.tensor_copy(table[0:1, 1:1 + OVER], ot[0:1, 1, :]).then_inc(table_ready, 1)
            dve.wait_ge(sct_done, 1)
            nc.vector.tensor_copy(sc[:, :], ps_sc).then_inc(sc_ready, 1)

            dve.wait_ge(table_ready, 1)
            jobs = dve.value_load(table[0:1, 0:1], min_val=E, max_val=E + OVER)
            with dve.Fori(0, jobs) as job:
                for u in range(UNITS):
                    n = job * UNITS + u
                    dve.wait_ge(hT_done, n + 1)
                    nc.vector.tensor_copy(h_T, ps_t[:, :]).then_inc(hT_ready, 1)
                    if u == 0:
                        dve.wait_ge(sct_done, job + 1)
                        select(job + 1).then_inc(sel_ready, 1)
                        dve.wait_ge(sel_ready, job + 2)
                        select_gated(job + 1).then_inc(selg_ready, 1)
                    else:
                        dve.wait_ge(gather_done, job + 2)
                        nc.vector.tensor_copy(xg[:, 5:8, :], gathered(7, 3)).then_inc(xg_ready, 1)
                    dve.wait_ge(chunk_used, n * RING + RING)
                    nc.vector.tensor_copy(y_s[:, HALF:D], ps_y[1][:, :]).then_inc(y_ready[1], 1)
                for d in range(2):
                    dve.wait_ge(scat_done[d], job * UNITS + UNITS)
                dve.wait_ge(sct_done, job + 2)
                nc.vector.tensor_copy(sc[:, :], ps_sc).then_inc(sc_ready, 1)
            dve.wait_ge(scat_done[1], jobs * UNITS)
            nc.vector.tensor_copy(out_s[:, HALF:D], ps_o[1][0:N, :]).then_inc(out_ready[1], 1)

        @block.tensor
        def _(pe):
            mm = nc.tensor.matmul

            def chunk_tile(g, k):
                return slot(gslot(g)).rearrange("p (k n) -> p k n", k=KT)[:, k, :]

            def project_T(m, actT, out_banks, chunks=range(GC)):
                for h in chunks:
                    g = GC * m + h
                    pe.wait_ge(gnn_in[g], 16)
                    for t in range(2):
                        c = P * (2 * (h % 2) + t)
                        for k in range(KT):
                            last = mm(bank[out_banks[h // 2]][:, c:c + N], chunk_tile(g, k)[:, P * t:P * t + P],
                                      actT[:, k, :], start=(k == 0), stop=(k == KT - 1))
                    last.then_inc(gnn_used, 1)

            def project(m, actT):
                for h in range(GC):
                    g = GC * m + h
                    pe.wait_ge(gnn_in[g], 16)
                    c = CW * (h % 2)
                    for k in range(KT):
                        last = mm(bank[2 + h // 2][0:N, c:c + CW], actT[:, k, :], chunk_tile(g, k), start=(k == 0),
                                  stop=(k == KT - 1))
                    last.then_inc(gnn_used, 1)

            def transposes(src, dst_banks, rows_in, done, src_ready):
                for b in range(2):
                    pe.wait_ge(src_ready, b + 1)
                    for t in range(4):
                        last = nc.tensor.transpose(bank[dst_banks[b]][:, P * t:P * t + rows_in],
                                                   src[:, P * (4 * b + t):P * (4 * b + t + 1)], ident[0:N, 0:N])
                    last.then_inc(done, 1)

            def map_groups(groups):
                for g in groups:
                    b = bank[g % 4]
                    if g >= 4:
                        pe.wait_ge(map_read, g - 3)
                    for t in range(g * EG, min(EC, g * EG + EG)):
                        c = (t - g * EG) * N
                        last = mm(b[0:N, c:c + N], src1h[:, t, :], dst1h[:, t, :], start=True, stop=True)
                    last.then_inc(map_done, 1)

            pe.wait_ge(const_ready, 6)
            transposes(xn, (0, 1), N, xT_done, xn_ready)
            pe.wait_ge(xT_ready, 2)
            project_T(Q, xT, (2, 3), (0,))
            pe.wait_ge(rows_ready, 1)
            for g in range(NG):
                if g % 2 == 0 and g:
                    project_T(Q, xT, (2, 3), (g // 2,))
                a, n = g * EG, min(EG, EC - g * EG)
                if g >= 2:
                    pe.wait_ge(same_done, g - 1)
                mm(bank[g % 2][0:N, 0:n * N], pair16[:, :], rows16[:, a * N:(a + n) * N], start=True,
                   stop=True).then_inc(cell_done, 1)
            project_T(K, xT, (4, 5))
            pe.wait_ge(same_done, NG)
            pe.wait_ge(code_ready, 1)
            pe.wait_ge(proj_read, 2)
            map_groups(range(4))
            project_T(Q2, qvT, (6, 7), (0,))
            map_groups(range(4, NG))
            project_T(Q2, qvT, (6, 7), (1, 2, 3))
            pe.wait_ge(proj_read, 4)
            pe.wait_ge(map_read, NG)
            project_T(K2, koT, (2, 3))
            project_T(V, xT, (4, 5))
            pe.wait_ge(proj_read, 8)
            for b in range(4):
                for c in range(4):
                    h = 8 * (b // 2) + 2 * c + b % 2
                    r = slice(HD * (h % 2), HD * (h % 2) + HD)
                    last = mm(bank[(0, 1, 6, 7)[b]][0:N, P * c:P * c + N], q2T[r, h // 2, :], k2T[r, h // 2, :],
                              start=True, stop=True)
                last.then_inc(score_done, 1)
            pe.wait_ge(proj_read, 10)
            project(V2, qvT)
            for b in range(4):
                pe.wait_ge(probs_ready, b + 1)
                for c in range(4):
                    last = nc.tensor.transpose(bank[(0, 1, 6, 7)[b]][0:N, P * c:P * c + N], probs[:, 4 * b + c, :],
                                               ident[0:N, 0:N])
                last.then_inc(probsT_done, 1)
            pe.wait_ge(v2_ready, 2)
            for half in range(2):
                for par in range(2):
                    b = 2 * half + par
                    pe.wait_ge(probsT_ready, b + 1)
                    for c in range(4):
                        h = 8 * half + 2 * c + par
                        last = mm(bank[4 + half][HD * par:HD * par + HD, P * c:P * c + N],
                                  v2[:, HD * h:HD * h + HD], probsT[:, 4 * b + c, :], start=True, stop=True)
                last.then_inc(pv_done, 1)
            pe.wait_ge(oT_ready, 2)
            project(O, koT)
            pe.wait_ge(x2_ready, 2)
            for h in range(2):
                mm(ps_o[h][0:N, :], ident[0:N, 0:N], x2[:, h * HALF:(h + 1) * HALF], start=True, stop=False,
                   skip_group_check=True)
            transposes(xn, (0, 1), N, x3T_done, x3_ready)
            pe.wait_ge(x3T_ready, 2)
            pe.wait_ge(gate_in, 16)
            pe.wait_ge(const_ready, 8)
            for k in range(KT):
                last = mm(bank[6][0:N, 0:N], xT[:, k, :], gate_w[:, k * E:k * E + N], start=(k == 0), stop=(k == KT - 1))
            last.then_inc(logit_done, 1)
            pe.wait_ge(chosen_ready, 1)
            mm(bank[2][0:N, 0:E], upper[:, :], chosen, start=True, stop=True).then_inc(rank_done, 1)
            mm(bank[3][0:N, 0:E], ones[:, :], chosen, start=True, stop=True).then_inc(count_done, 1)

            def gather():
                for k in range(KT):
                    b, c = gather_at[k]
                    last = mm(bank[b][:, c:c + N], xn[:, k * P:(k + 1) * P], sel, start=True, stop=True)
                last.then_inc(gather_done, 1)

            def scatter_matrix():
                mm(ps_sc, selg.rearrange("p c s -> p (c s)"), ident[0:N, 0:N], start=True,
                   stop=True).then_inc(sct_done, 1)

            def unit(job, u, slots, landed):
                n = job * UNITS + u
                if u == 0:
                    pe.wait_ge(xg_ready, job * 2 + 2)
                for k in range(W1C):
                    pe.wait_ge(ring_in[slots[k]], landed[k])
                    w = slot(slots[k])
                    for j in range(4):
                        last = mm(ps_h[SLOTS * j:SLOTS * (j + 1), :], xg[:, k, :], w[:, HALF * j:HALF * (j + 1)],
                                  start=(k == 0), stop=(k == W1C - 1))
                    last.then_inc(chunk_used, 1)
                if u == 0 and isinstance(job, int):
                    pe.wait_ge(selg_ready, 1)
                    scatter_matrix()
                pe.wait_ge(h_ready, n + 1)
                for c in range(CT):
                    last = nc.tensor.transpose(ps_t[:, P * c:P * c + P], h_s[:, P * c:P * c + P], ident[:, :])
                last.then_inc(hT_done, 1)
                if u == UNITS - 1:
                    pe.wait_ge(selg_ready, job + 2)
                    pe.wait_ge(sc_ready, job + 1)
                    scatter_matrix()
                    pe.wait_ge(sel_ready, job + 2)
                    gather()
                pe.wait_ge(hT_ready, n + 1)

                def scatter(d):
                    pe.wait_ge(y_ready[d], n + 1)
                    mm(ps_o[d][0:N, :], sc[:, :], y_s[:, HALF * d:HALF * (d + 1)], start=False, stop=False,
                       skip_group_check=True).then_inc(scat_done[d], 1)

                for i in range(W2C):
                    d, c = i // CT, i % CT
                    pe.wait_ge(ring_in[slots[W1C + i]], landed[W1C + i])
                    w = slot(slots[W1C + i]).rearrange("p (j d) -> p j d", d=HALF)
                    for j in range(4):
                        last = mm(ps_y[d][SLOTS * j:SLOTS * (j + 1), :], h_T[:, P * c + SLOTS * j:P * c + SLOTS * (j + 1)],
                                  w[:, j, :], start=(c == 0), stop=(c == CT - 1))
                    last.then_inc(chunk_used, 1)
                    if i == CT + 1:
                        if u == 0:
                            pe.wait_ge(sc_ready, job + 1)
                        scatter(0)
                scatter(1)

            pe.wait_ge(sel_ready, 1)
            gather()
            for u in range(UNITS):
                order = range(RING * u, RING * (u + 1))
                unit(0, u, [first_slot(c) for c in order], [16 * (c // SLOTS_ALL + 1) for c in order])
            pe.wait_ge(table_ready, 1)
            jobs = pe.value_load(table[0:1, 0:1], min_val=E, max_val=E + OVER)
            with pe.Fori(1, jobs) as job:
                for u in range(UNITS):
                    n = job * UNITS + u
                    unit(job, u, range(RING), [n * 16 + (16 if c < AGAIN else 0) for c in range(RING)])


def _col_layout(w):
    return w.T.reshape(KT, P, GC, CW).transpose(2, 1, 0, 3).reshape(GC, P, CHUNK)


def _layout(a):
    w = {k: np.asarray(v) for k, v in a.items()}
    g = {k[7:]: v for k, v in w.items() if k.startswith("L0_gnn_")}
    gnn = np.concatenate([_col_layout(g[k]) for k in ("wq", "wk", "wiq", "wik", "wv", "wiv", "wo")])
    colb = np.stack([g[k] for k in ("bq", "bk", "biq", "bik", "bv")]).reshape(5, KT, P).transpose(2, 0, 1)
    edges = np.stack([w["src"], w["dst"], w["edge_type_5"]])
    w1 = w["L0_ffn_w1"].reshape(E, UNITS, UF, KT, P).transpose(0, 1, 3, 4, 2)
    w2 = w["L0_ffn_w2"].reshape(E, 2, HALF, UNITS, 4, CT, P).transpose(0, 3, 1, 5, 6, 4, 2)
    return {
        "x": w["x"],
        "rows": edges[0:2],
        "cols": edges.reshape(3, EC, N).transpose(2, 0, 1),
        "etw": g["edge_type_weights"].reshape(1, 4),
        "gnn_w": gnn,
        "colb": colb,
        "biv": g["biv"].reshape(1, D),
        "bo": g["bo"].reshape(1, D),
        "gate": w["L0_ffn_gate_w"].T.reshape(KT, P, E).transpose(1, 0, 2).reshape(P, KT * E),
        "w1": w1.reshape(E, UNITS, W1C, P, CHUNK),
        "w2": w2.reshape(E, UNITS, W2C, P, CHUNK),
    }


def kernel(**inputs):
    import concourse.bacc as bacc
    from concourse.bass_utils import run_bass_kernel_spmd

    nc = bacc.Bacc("TRN2", target_bir_lowering=False, num_devices=1)
    arrays, args = {}, []
    for name, a in _layout(inputs).items():
        a = np.ascontiguousarray(a)
        arrays[f"in_{name}"] = a
        args.append(nc.dram_tensor(f"in_{name}", a.shape, mybir.dt.from_np(a.dtype), kind="ExternalInput").ap())
    out = nc.dram_tensor("out_0", (N, D), F32, kind="ExternalOutput").ap()
    gnn_moe_kernel(nc, *args, out)
    r = run_bass_kernel_spmd(nc, [arrays], core_ids=[0])
    return r.results[0]["out_0"]
```
